# Optimizing a Trainium2 kernel written in Bass

```python
import numpy as np
import jax
import jax.numpy as jnp

def _softmax(x, axis=-1):
    return jax.nn.softmax(x, axis=axis)

def _gelu(x):
    return jax.nn.gelu(x, approximate=True)

def _silu(x):
    return jax.nn.silu(x)

def _sigmoid(x):
    return jax.nn.sigmoid(x)

def _layernorm(x, axis=-1, eps=1e-05):
    m = jnp.mean(x, axis=axis, keepdims=True)
    v = jnp.var(x, axis=axis, keepdims=True)
    return (x - m) / jnp.sqrt(v + eps)

def _scatter_add(tgt, idx, src, axis=0):
    return tgt.at[idx].add(src)

def _segment_sum(src, seg, n):
    return jax.ops.segment_sum(src, seg, n)
kernel_name = 'mk_cond_resid_d2_seqx_r2_0ab7ac'

def setup_inputs(seed: int=0):
    np.random.seed(seed)
    _w = jnp.asarray

    def _rec_inputs():
        import jax
        import jax.numpy as jnp
        _rk = jax.random.key(seed)
        x = -0.0002071 + 1 * jax.random.normal(jax.random.fold_in(_rk, 1), (32, 128, 512), jnp.float32)
        _lenS = 128 - jax.random.randint(jax.random.fold_in(_rk, 7), (32,), 0, max(1, 128 // 4) + 1, jnp.int32)
        _lenS2 = 128 - jax.random.randint(jax.random.fold_in(_rk, 8), (32,), 0, max(1, 128 // 4) + 1, jnp.int32)
        cond_8 = jax.random.uniform(jax.random.fold_in(_rk, 11), (32, 8), jnp.float32, 0.0, 0.983423)
        return (x, cond_8)
    x, cond_8 = _rec_inputs()

    def _L0_cond_setup():
        import jax, jax.numpy as jnp
        import numpy as np
        R = 16
        ALPHA = 32.0
        SCALING = ALPHA / R
        key = jax.random.key(seed)
        ks = jax.random.split(key, 6)
        B, T, C, O, E = (16, 750, 512, 512, 8)
        x = jax.random.normal(ks[0], (B, T, C), dtype=jnp.float32)
        w = jax.random.uniform(ks[1], (B, E), dtype=jnp.float32)
        W_base = jax.random.normal(ks[2], (O, C), dtype=jnp.float32) * 0.02
        b_base = jax.random.normal(ks[3], (O,), dtype=jnp.float32) * 0.02
        As = jax.random.normal(ks[4], (E, R, C), dtype=jnp.float32) * 0.02
        Bs = jax.random.normal(ks[5], (E, O, R), dtype=jnp.float32) * 0.02
        return {'x': x, 'w': w, 'W_base': W_base, 'b_base': b_base, 'As': As, 'Bs': Bs}
    _L0_cond_all = _L0_cond_setup()
    _L0_cond_in = {k: v for k, v in _L0_cond_all.items() if k in ('W_base', 'b_base', 'As', 'Bs')}
    del _L0_cond_all

    def _L1_cond_setup():
        import jax, jax.numpy as jnp
        import numpy as np
        B, S, D = (16, 1024, 512)
        E, H = (8, 1024)
        key = jax.random.key(seed)
        ks = jax.random.split(key, 8)
        scale = 0.02
        x = jax.random.normal(ks[0], (B, S, D), dtype=jnp.float32)
        opcode_onehot = jax.random.uniform(ks[1], (B, E), dtype=jnp.float32)
        W_up = jax.random.normal(ks[2], (E, H, D), dtype=jnp.float32) * scale
        b_up = jnp.zeros((E, H), dtype=jnp.float32)
        W_gate = jax.random.normal(ks[3], (E, H, D), dtype=jnp.float32) * scale
        b_gate = jnp.zeros((E, H), dtype=jnp.float32)
        W_down = jax.random.normal(ks[4], (E, D, H), dtype=jnp.float32) * scale
        b_down = jnp.zeros((E, D), dtype=jnp.float32)
        return {'x': x, 'opcode_onehot': opcode_onehot, 'W_up': W_up, 'b_up': b_up, 'W_gate': W_gate, 'b_gate': b_gate, 'W_down': W_down, 'b_down': b_down}
    _L1_cond_all = _L1_cond_setup()
    _L1_cond_in = {k: v for k, v in _L1_cond_all.items() if k in ('W_up', 'b_up', 'W_gate', 'b_gate', 'W_down', 'b_down')}
    del _L1_cond_all
    return {'x': x, 'cond_8': cond_8, 'L0_cond_W_base': _L0_cond_in['W_base'], 'L0_cond_b_base': _L0_cond_in['b_base'], 'L0_cond_As': _L0_cond_in['As'], 'L0_cond_Bs': _L0_cond_in['Bs'], 'L1_cond_W_up': _L1_cond_in['W_up'], 'L1_cond_b_up': _L1_cond_in['b_up'], 'L1_cond_W_gate': _L1_cond_in['W_gate'], 'L1_cond_b_gate': _L1_cond_in['b_gate'], 'L1_cond_W_down': _L1_cond_in['W_down'], 'L1_cond_b_down': _L1_cond_in['b_down']}

def reference(x, cond_8, L0_cond_W_base, L0_cond_b_base, L0_cond_As, L0_cond_Bs, L1_cond_W_up, L1_cond_b_up, L1_cond_W_gate, L1_cond_b_gate, L1_cond_W_down, L1_cond_b_down):
    import jax
    import jax.numpy as jnp

    def _L0_cond_ref(x, w, W_base, b_base, As, Bs):
        import jax, jax.numpy as jnp
        import numpy as np
        R = 16
        ALPHA = 32.0
        SCALING = ALPHA / R
        out = jnp.einsum('btc,oc->bto', x, W_base) + b_base
        h = jnp.einsum('btc,erc->bter', x, As)
        lora = jnp.einsum('bter,eor,be->bto', h, Bs, w)
        return out + lora * SCALING

    def _L1_cond_ref(x, opcode_onehot, W_up, b_up, W_gate, b_gate, W_down, b_down):
        import jax, jax.numpy as jnp
        import numpy as np
        B, S, D = (16, 1024, 512)
        E, H = (8, 1024)
        expert = jnp.argmax(opcode_onehot, axis=-1)
        wu, bu = (W_up[expert], b_up[expert])
        wg, bg = (W_gate[expert], b_gate[expert])
        wd, bd = (W_down[expert], b_down[expert])
        up = jnp.einsum('bsd,bhd->bsh', x, wu) + bu[:, None, :]
        gate = jnp.einsum('bsd,bhd->bsh', x, wg) + bg[:, None, :]
        hidden = jax.nn.silu(up) * gate
        out = jnp.einsum('bsh,bdh->bsd', hidden, wd) + bd[:, None, :]
        return out
    x = x + _L0_cond_ref(x, cond_8, L0_cond_W_base, L0_cond_b_base, L0_cond_As, L0_cond_Bs)
    x = x + _L1_cond_ref(x, cond_8, L1_cond_W_up, L1_cond_b_up, L1_cond_W_gate, L1_cond_b_gate, L1_cond_W_down, L1_cond_b_down)
    return x

_drawn_inputs = setup_inputs


def setup_inputs(seed=0):
    import zlib

    import numpy as np

    out = dict(_drawn_inputs(seed))
    spreads = {'L1_cond_b_up': (0.0, 0.495), 'L1_cond_b_gate': (0.0, 0.506), 'L1_cond_b_down': (0.0, 0.1)}
    factors = {'L0_cond_b_base': 3.326}
    for name, (base, spread) in spreads.items():
        noise = np.random.default_rng([zlib.crc32(name.encode()), seed]).standard_normal(out[name].shape)
        drawn = base * np.exp(spread * noise) if base else spread * noise
        out[name] = jnp.asarray(drawn.astype(out[name].dtype))
    for name, factor in factors.items():
        out[name] = (out[name] * factor).astype(out[name].dtype)
    return out
```

```python
from contextlib import ExitStack

import concourse.bass as bass
from concourse import mybir

F32 = mybir.dt.float32
F32R = mybir.dt.float32r
I32 = mybir.dt.int32
ACT = mybir.ActivationFunctionType
ALU = mybir.AluOpType
AX_X = mybir.AxisListType.X

P = 128
B, S, D = 32, 128, 512
E, H, R = 8, 1024, 16
KD = D // P
KH = H // P
N = 512
GS = N // S
G = B // GS
LORA_SCALE = 2.0

ER = E * R
L0C = ER + D
L0W = KD * L0C + D
BLOCKS = 2 * KD * (H // N) + KH
CH = 2 * N
CHUNKS = BLOCKS // 2
UG = 8
DN = CHUNKS - UG
RING = 6
RING0 = 4
BIAS = 5 * N

T_SAMPLE, T_CHANGED, T_RUN, T_EXPERT, T_RUNS, T_LEN = 0, 32, 64, 96, 104, 112


def program(nc, x_t, cond_row, cond_t, l0_w, l0_b, l1_w, l1_b, out):
    assert ER == P and S == P and G == 8 and CHUNKS == 12
    x1_dram = nc.dram_tensor("x1_scratch", (B, P, KD * S), F32, kind="Internal").ap()

    with ExitStack() as ctx:
        at = [(nc.sbuf_base + 31) // 32 * 32]

        def place(name, cols, dt=F32, offset=None, parts=P):
            if offset is None:
                offset = at[0]
                at[0] += (4 * cols + 31) // 32 * 32
            return nc.alloc_sbuf_tensor_at(name, [parts, cols], dt, offset=offset)

        def sem(name):
            return ctx.enter_context(nc.semaphore(name))

        def over(tensor_at, name, sizes, dt=F32):
            made = []
            for n, cols in enumerate(sizes):
                made.append(place(f"{name}{n}", cols, dt, offset=tensor_at))
                tensor_at += 4 * cols
            return made

        w_hi = place("w_hi", BLOCKS * N, F32R)
        w_lo_at = at[0]
        w_lo = place("w_lo", BLOCKS * N, F32R)
        raw = place("raw", RING * CH)
        bias_at = at[0]
        bias = place("bias", 2 * BIAS)
        ident = place("ident", P)
        lora_w = place("lora_w", B)
        base_b = place("base_b", KD)
        table = place("table", T_LEN, I32)
        l0_hi = place("l0_hi", L0W, F32R)
        l0_lo = place("l0_lo", L0W, F32R)
        xg_at = at[0]
        xg = [place(f"xg{n}", GS * D) for n in range(2)]
        xs_at = at[0]
        x_hi = place("x_hi", GS * D, F32R)
        x_lo = place("x_lo", GS * D, F32R)
        hs_at = at[0]
        low = place("low", N)
        low_hi = place("low_hi", N, F32R)
        low_lo = place("low_lo", N, F32R)
        assert at[0] <= nc.sbuf_usable_end, (at[0], nc.sbuf_usable_end)
        l0_raw = place("l0_raw", L0W, offset=w_lo_at + 4 * (BLOCKS * N - L0W))
        wide = [place(f"wide{n}", B * B, offset=bias_at + 4 * (BIAS + n * B * B), parts=1) for n in range(2)]
        rows = place("rows", 13 * B, parts=1)
        rows_i = place("rows_i", 4 * B, I32, parts=1)
        assert at[0] <= nc.sbuf_usable_end, (at[0], nc.sbuf_usable_end)
        x1 = over(xg_at, "x1_", [D, D])
        pre, act_up, gate, resid = over(xg_at + 4 * 2 * D, "row_", [N, N, N, D])
        hidden = over(xg_at + 4 * (2 * D + 4 * N), "hidden", [N, N])
        x1_split = over(xs_at, "x1_split", [2 * D, 2 * D], F32R)
        hid_hi, hid_lo = over(xs_at + 4 * 4 * D, "hid_split", [H, H], F32R)
        result = over(hs_at, "result", [D, D])

        bank = [ctx.enter_context(nc.psum_tensor(f"bank{n}", [P, N], F32)) for n in range(8)]
        q_ps, t_ps, r_ps, d_ps = bank[0:4], bank[4:6], bank[6], bank[7]
        low_ps = bank[4]

        cond_loaded, lora_w_loaded, base_b_loaded = sem("cond_loaded"), sem("lora_w_loaded"), sem("base_b_loaded")
        l0_loaded = [sem(f"l0_loaded{n}") for n in range(KD + 1)]
        l0_hi_ready, l0_lo_ready = sem("l0_hi_ready"), sem("l0_lo_ready")
        iota_ready, ident_ready, table_step, table_ready = sem("iota_ready"), sem("ident_ready"), sem("table_step"), sem("table_ready")
        x_loaded = [sem(f"x_loaded{n}") for n in range(2)]
        x_hi_ready, x_lo_ready, x_used = sem("x_hi_ready"), sem("x_lo_ready"), sem("x_used")
        low_done, low_scaled, low_hi_ready, low_lo_ready = sem("low_done"), sem("low_scaled"), sem("low_hi_ready"), sem("low_lo_ready")
        base_done, x1_made = sem("base_done"), sem("x1_made")
        x1_stored = [sem(f"x1_stored{n}") for n in range(2)]
        raw_loaded = [sem(f"raw_loaded{n}") for n in range(RING)]
        bias_loaded = sem("bias_loaded")
        w_hi_ready, raw_free, copy_go = sem("w_hi_ready"), sem("raw_free"), sem("copy_go")
        ug_ready, ug_used, down_ready, down_used = sem("ug_ready"), sem("ug_used"), sem("down_ready"), sem("down_used")
        x1_loaded = [sem(f"x1_loaded{n}") for n in range(2)]
        x1_hi_ready, x1_lo_ready = sem("x1_hi_ready"), sem("x1_lo_ready")
        q_read, silu_ready, h_ready = sem("q_read"), sem("silu_ready"), sem("h_ready")
        t_done, hid_hi_ready, hid_lo_ready = sem("t_done"), sem("hid_hi_ready"), sem("hid_lo_ready")
        r_done, resid_ready, result_ready = sem("r_done"), sem("resid_ready"), sem("result_ready")
        stored = [sem(f"stored{n}") for n in range(2)]

        block = ctx.enter_context(nc.Block())

        def l0_piece(n):
            return slice(n * L0C, min((n + 1) * L0C, L0W))

        def xk(buf, k):
            return buf[:, :].rearrange("p (s k t) -> p s k t", s=GS, k=KD)[:, :, k, :]

        def chunk(buf, c):
            return buf[:, c * CH:(c + 1) * CH]

        def entry(eng, column, index, high):
            return eng.value_load(table[0:1, bass.ds(index + column, 1)], min_val=0, max_val=high)

        @block.sync
        def _(sp):
            sp.dma_start(l0_raw[:, l0_piece(0)], l0_w[:, l0_piece(0)]).then_inc(l0_loaded[0], 16)
            sp.dma_start(xg[0][:, :], x_t[0]).then_inc(x_loaded[0], 16)
            for n in range(1, KD + 1):
                sp.dma_start(l0_raw[:, l0_piece(n)], l0_w[:, l0_piece(n)]).then_inc(l0_loaded[n], 16)
            sp.dma_start(xg[1][:, :], x_t[1]).then_inc(x_loaded[1], 16)

            def load_chunk(run_expert, c, slot):
                sp.dma_start(chunk(raw, slot),
                             l1_w[bass.ds(run_expert, 1), :, c * CH:(c + 1) * CH].rearrange("a p n -> p (a n)"))\
                  .then_inc(raw_loaded[slot], 16)

            def load_bias(run_expert, offset):
                row = l1_b[bass.ds(run_expert, 1), :].to_broadcast([P, BIAS])
                sp.dma_start(bias[:, bass.ds(offset, BIAS)], row).then_inc(bias_loaded, 16)

            def load_x(g, n):
                sp.wait_ge(x1_stored[n], (g - n) * 8)
                sp.dma_start(xg[n][:, :], x_t[bass.ds(g, 1)].rearrange("a p n -> p (a n)")).then_inc(x_loaded[n], 16)

            sp.wait_ge(table_ready, 1)
            first = entry(sp, T_EXPERT, 0, E - 1)
            for c in range(RING0):
                load_chunk(first, c, c)
            load_bias(first, 0)
            load_x(2, 0)
            load_x(3, 1)
            for i in range(1, CHUNKS // RING0):
                for n in range(RING0):
                    c = RING0 * i + n
                    sp.wait_ge(raw_free, c - RING0 + 1)
                    load_chunk(first, c, n)
                load_x(2 * i + 2, 0)
                load_x(2 * i + 3, 1)
            runs = entry(sp, T_RUNS, 0, E)
            with sp.Fori(1, E) as r:
                with sp.If(runs > r):
                    expert = entry(sp, T_EXPERT, r, E - 1)
                    sp.wait_ge(raw_free, r * CHUNKS)
                    for c in range(RING):
                        load_chunk(expert, c, c)
                    sp.wait_ge(bias_loaded, r * 16)
                    load_bias(expert, (r % 2) * BIAS)
                    for c in range(RING, CHUNKS):
                        sp.wait_ge(raw_free, r * CHUNKS + c - RING + 1)
                        load_chunk(expert, c, c - RING)

        @block.gpsimd
        def _(pool):
            nc.gpsimd.iota(rows_i[0:1, 0:E], pattern=[[-1, E]], base=E, channel_multiplier=0).then_inc(iota_ready, 1)
            nc.gpsimd.iota(rows_i[0:1, B:2 * B], pattern=[[1, B]], base=0, channel_multiplier=0).then_inc(iota_ready, 1)
            nc.gpsimd.memset(ident[:, :], 0.0).then_inc(ident_ready, 1)
            pool.wait_ge(ident_ready, 1)
            nc.gpsimd.affine_select(out=ident[:, :], in_=ident[:, :], compare_op=ALU.not_equal, fill=1.0, base=0,
                                    pattern=[[-1, P]], channel_multiplier=1).then_inc(ident_ready, 1)

            with pool.Fori(0, CHUNKS // RING0) as i:
                for n in range(RING0):
                    pool.wait_ge(raw_loaded[n], i * 16 + 16)
                    pool.sem_inc(copy_go, 1)
                    nc.gpsimd.tensor_copy(w_hi[:, bass.ds(i * (RING0 * CH) + n * CH, CH)], chunk(raw, n)).then_inc(w_hi_ready, 1)

            def high(c, runs_before):
                loads = (CHUNKS // RING0 if c % RING < RING0 else 0) + c // RING + 1
                pool.wait_ge(raw_loaded[c % RING], runs_before * 32 + 16 * loads)
                pool.sem_inc(copy_go, 1)
                nc.gpsimd.tensor_copy(chunk(w_hi, c), chunk(raw, c % RING)).then_inc(w_hi_ready, 1)

            def step(s, first=False, last=False):
                if not first:
                    changed = entry(pool, T_CHANGED, s, 1)
                    with pool.If(changed > 0):
                        run = entry(pool, T_RUN, s - 1, E - 1)
                        for n in range(DN):
                            pool.wait_ge(down_used, s * DN + (n + 1 - DN))
                            high(UG + n, run)
                if not last:
                    changed = entry(pool, T_CHANGED, s + 1, 1)
                    with pool.If(changed > 0):
                        run = entry(pool, T_RUN, s, E - 1)
                        for c in range(UG):
                            pool.wait_ge(ug_used, s * UG + (c + 1))
                            high(c, run)

            pool.wait_ge(table_ready, 1)
            step(0, first=True)
            with pool.Fori(1, B - 1) as s:
                step(s)
            step(B - 1, last=True)

        @block.scalar
        def _(act):
            act.dma_start(rows[0:1, 0:B * E], cond_row).then_inc(cond_loaded, 16)
            act.dma_start(lora_w[:, :], cond_t).then_inc(lora_w_loaded, 16)
            act.dma_start(base_b[:, :], l0_b).then_inc(base_b_loaded, 16)

            def x_high(g, n, k):
                nc.scalar.activation(xk(x_hi, k), xk(xg[n], k), ACT.Copy).then_inc(x_hi_ready, 1)

            def l0_high(n):
                act.wait_ge(l0_loaded[n], 16)
                nc.scalar.activation(l0_hi[:, l0_piece(n)], l0_raw[:, l0_piece(n)], ACT.Copy).then_inc(l0_hi_ready, 1)

            def next_x_high(g, n, k):
                if k == 0:
                    act.wait_ge(x_loaded[1 - n], (g + n) * 8 + 16)
                act.wait_ge(x_used, g * KD + (k + 1))
                x_high(g + 1, 1 - n, k)

            def group(g, n, last=False):
                if not last:
                    for k in range(KD - 1):
                        next_x_high(g, n, k)
                act.wait_ge(low_scaled, g + 1)
                nc.scalar.activation(low_hi[:, :], low[:, :], ACT.Copy).then_inc(low_hi_ready, 1)
                if not last:
                    next_x_high(g, n, KD - 1)
                act.wait_ge(x1_made, g * KD + KD)
                act.dma_start(x1_dram[bass.ds(g * GS, GS)].rearrange("s p n -> p s n"),
                              xg[n][:, :].rearrange("p (s n) -> p s n", s=GS)).then_inc(x1_stored[n], 16)

            l0_high(0)
            act.wait_ge(x_loaded[0], 16)
            x_high(0, 0, 0)
            for k in range(1, KD):
                l0_high(k)
                x_high(0, 0, k)
            l0_high(KD)
            group(0, 0)
            with act.Fori(0, (G - 2) // 2) as i:
                group(i * 2 + 1, 1)
                group(i * 2 + 2, 0)
            group(G - 1, 1, last=True)

            act.sem_inc(stored[0], 16)
            act.sem_inc(stored[1], 16)

            def load_x1(s, n):
                sample = entry(act, T_SAMPLE, s, B - 1)
                act.dma_start(x1[n][:, :], x1_dram[bass.ds(sample, 1)].rearrange("a p n -> p (a n)")).then_inc(x1_loaded[n], 16)

            def x1_high(s, n):
                act.wait_ge(x1_loaded[n], (s - n) * 8 + 16)
                nc.scalar.activation(x1_split[n][:, 0:D], x1[n][:, :], ACT.Copy).then_inc(x1_hi_ready, 1)

            def hidden_high(s, half):
                act.wait_ge(t_done, s * 2 + (half + 1))
                cols = slice(half * N, (half + 1) * N)
                nc.scalar.activation(hid_hi[:, cols], t_ps[half][:, :], ACT.Copy).then_inc(hid_hi_ready, 1)

            def silu(s, half, free):
                act.wait_ge(q_read, s * 4 + (2 * half + 1))
                if free:
                    act.wait_ge(h_ready, s * 2 + half)
                nc.scalar.activation(act_up[:, :], pre[:, :], ACT.Silu).then_inc(silu_ready, 1)

            def store(s, n):
                sample = entry(act, T_SAMPLE, s, B - 1)
                act.wait_ge(result_ready, s + 1)
                act.dma_start(out[bass.ds(sample, 1)].rearrange("a t d -> t (a d)"), result[n][:, :]).then_inc(stored[n], 16)

            def step(s, n, first=False, last=False):
                if not first:
                    hidden_high(s - 1, 1)
                silu(s, 0, not first)
                if not last:
                    if not first:
                        act.wait_ge(r_done, s)
                        act.wait_ge(ug_used, s * UG)
                    load_x1(s + 1, 1 - n)
                if not first:
                    store(s - 1, 1 - n)
                silu(s, 1, True)
                hidden_high(s, 0)
                if not last:
                    x1_high(s + 1, 1 - n)

            act.wait_ge(x1_stored[0], 16 * G // 2)
            act.wait_ge(x1_stored[1], 16 * G // 2)
            load_x1(0, 0)
            x1_high(0, 0)
            step(0, 0, first=True)
            step(1, 1)
            with act.Fori(1, B // 2 - 1) as i:
                step(i * 2, 0)
                step(i * 2 + 1, 1)
            step(B - 2, 0)
            step(B - 1, 1, last=True)
            hidden_high(B - 1, 1)
            store(B - 1, 1)
            act.wait_ge(stored[0], 16 + 16 * B // 2)
            act.wait_ge(stored[1], 16 + 16 * B // 2)

        @block.vector
        def _(dve):
            def sort_samples():
                done = [0]

                def then(instruction):
                    done[0] += 1
                    instruction.then_inc(table_step, 1)
                    dve.wait_ge(table_step, done[0])

                cond = rows[0:1, 0:B * E]
                row = lambda n: rows[0:1, (8 + n) * B:(9 + n) * B]
                square = lambda buf, a=B, b=B: buf[0:1, 0:a * b].rearrange("p (a b) -> p a b", a=a)
                outer = lambda r, a=B, b=B: r.unsqueeze(2).to_broadcast([1, a, b])
                inner = lambda r, a=B, b=B: r.unsqueeze(1).to_broadcast([1, a, b])
                spare, key, rank, index = row(0), row(1), row(2), row(3)
                down8 = row(4)[:, 0:E]
                dve.wait_ge(iota_ready, 2)
                dve.wait_ge(cond_loaded, 16)
                then(nc.vector.tensor_copy(down8, rows_i[0:1, 0:E]))
                then(nc.vector.tensor_copy(index, rows_i[0:1, B:2 * B]))
                cond3 = cond.rearrange("p (b e) -> p b e", b=B)
                then(nc.vector.tensor_reduce(spare, cond3, AX_X, ALU.max))
                then(nc.vector.tensor_tensor(square(wide[0], B, E), cond3, outer(spare, B, E), ALU.is_ge))
                then(nc.vector.tensor_tensor(square(wide[1], B, E), square(wide[0], B, E), inner(down8, B, E), ALU.mult))
                then(nc.vector.tensor_reduce(spare, square(wide[1], B, E), AX_X, ALU.max))
                then(nc.vector.tensor_scalar(key, spare, 1.0, -float(B), ALU.max, ALU.mult))
                then(nc.vector.scalar_tensor_tensor(key, key, float(B * E), index, ALU.add, ALU.add))
                then(nc.vector.tensor_tensor(square(wide[0]), inner(key), outer(key), ALU.is_lt))
                then(nc.vector.tensor_reduce(rank, square(wide[0]), AX_X, ALU.add))
                then(nc.vector.tensor_tensor(square(wide[0]), outer(index), inner(rank), ALU.is_equal))
                then(nc.vector.tensor_tensor(square(wide[1]), square(wide[0]), inner(key), ALU.mult))
                then(nc.vector.tensor_reduce(spare, square(wide[1]), AX_X, ALU.add))
                keys_i, experts_i = rows_i[0:1, 2 * B:3 * B], rows_i[0:1, 3 * B:4 * B]
                then(nc.vector.tensor_copy(keys_i, spare))
                then(nc.vector.tensor_single_scalar(table[0:1, T_SAMPLE:T_SAMPLE + B], keys_i, B - 1, ALU.bitwise_and))
                then(nc.vector.tensor_single_scalar(experts_i, keys_i, 5, ALU.arith_shift_right))
                expert, changed, run = key, rank, spare
                then(nc.vector.tensor_copy(expert, experts_i))
                then(nc.vector.memset(changed, 0.0))
                then(nc.vector.tensor_tensor(changed[:, 1:B], expert[:, 1:B], expert[:, 0:B - 1], ALU.not_equal))
                then(nc.vector.tensor_copy(table[0:1, T_CHANGED:T_CHANGED + B], changed))
                then(nc.vector.tensor_tensor(square(wide[0]), inner(index), outer(index), ALU.is_le))
                then(nc.vector.tensor_tensor(square(wide[1]), square(wide[0]), inner(changed), ALU.mult))
                then(nc.vector.tensor_reduce(run, square(wide[1]), AX_X, ALU.add))
                then(nc.vector.tensor_copy(table[0:1, T_RUN:T_RUN + B], run))
                then(nc.vector.tensor_scalar(table[0:1, T_RUNS:T_RUNS + 1], run[:, B - 1:B], 1.0, None, ALU.add))
                then(nc.vector.tensor_tensor(square(wide[0], E, B), outer(index[:, 0:E], E, B), inner(run, E, B), ALU.is_equal))
                then(nc.vector.tensor_tensor(square(wide[1], E, B), square(wide[0], E, B), inner(expert, E, B), ALU.mult))
                then(nc.vector.tensor_reduce(rank[:, 0:E], square(wide[1], E, B), AX_X, ALU.max))
                nc.vector.tensor_copy(table[0:1, T_EXPERT:T_EXPERT + E], rank[:, 0:E]).then_inc(table_ready, 1)

            def subtract(lo, whole, hi):
                return nc.vector.tensor_tensor(lo, whole, hi.bitcast(F32), ALU.subtract)

            def l0_low(n):
                dve.wait_ge(l0_hi_ready, n + 1)
                subtract(l0_lo[:, l0_piece(n)], l0_raw[:, l0_piece(n)], l0_hi[:, l0_piece(n)]).then_inc(l0_lo_ready, 1)

            def x_low(g, n, k):
                dve.wait_ge(x_hi_ready, g * KD + (k + 1))
                subtract(xk(x_lo, k), xk(xg[n], k), xk(x_hi, k)).then_inc(x_lo_ready, 1)

            def w_low(c, slot, ready):
                at_c = bass.ds(c * CH, CH)
                subtract(w_lo[:, at_c], chunk(raw, slot), w_hi[:, at_c]).then_inc(ready, 1)

            def group(g, n, weights=None, first=False, last=False):
                if first:
                    sort_samples()
                if not last:
                    for k in range(KD - 1):
                        x_low(g + 1, 1 - n, k)
                        if weights is not None and k < 2:
                            weights(k)
                dve.wait_ge(low_done, g + 1)
                if not first:
                    dve.wait_ge(low_lo_ready, g)
                nc.vector.tensor_tensor(low[:, :].rearrange("p (s t) -> p s t", s=GS),
                                        low_ps[:, :].rearrange("p (s t) -> p s t", s=GS),
                                        lora_w[:, bass.ds(g * GS, GS)].unsqueeze(2).to_broadcast([P, GS, S]),
                                        ALU.mult).then_inc(low_scaled, 1)
                dve.wait_ge(low_hi_ready, g + 1)
                subtract(low_lo[:, :], low[:, :], low_hi[:, :]).then_inc(low_lo_ready, 1)
                if not last:
                    x_low(g + 1, 1 - n, KD - 1)
                for m in range(KD):
                    dve.wait_ge(base_done, g * KD + (m + 1))
                    nc.vector.scalar_tensor_tensor(xk(xg[n], m), q_ps[m][:, :].rearrange("p (s t) -> p s t", s=GS),
                                                   base_b[:, m:m + 1], xk(xg[n], m), ALU.add, ALU.add)\
                      .then_inc(x1_made, 1)

            for k in range(KD):
                l0_low(k)
                x_low(0, 0, k)
            l0_low(KD)
            dve.wait_ge(lora_w_loaded, 16)
            nc.vector.tensor_scalar(lora_w[:, :], lora_w[:, :], LORA_SCALE, None, ALU.mult).then_inc(lora_w_loaded, 1)
            dve.wait_ge(lora_w_loaded, 17)
            dve.wait_ge(base_b_loaded, 16)
            group(0, 0, first=True)

            def first_run(i, part, ready):
                def one(j):
                    n = 2 * part + j
                    dve.wait_ge(w_hi_ready, i * RING0 + (n + 1))
                    w_low(i * RING0 + n, n, ready)
                    dve.wait_ge(ready, (i * RING0 if ready is ug_ready else 0) + (n + 1))
                    dve.sem_inc(raw_free, 1)
                return one

            def pair(i, ready):
                group(i * 2 + 1, 1, weights=first_run(i, 0, ready))
                group(i * 2 + 2, 0, weights=first_run(i, 1, ready))

            with dve.Fori(0, UG // RING0) as i:
                pair(i, ug_ready)
            pair(UG // RING0, down_ready)
            group(G - 1, 1, last=True)

            def add_bias(s, q, dst, run, wait_bias=False):
                if wait_bias:
                    dve.wait_ge(bias_loaded, run * 16 + 16)
                dve.wait_ge(ug_used, s * UG + (2 * q + 2))
                nc.vector.tensor_tensor(dst[:, :], q_ps[q][:, :], bias[:, bass.ds((run % 2) * BIAS + q * N, N)], ALU.add)\
                  .then_inc(q_read, 1)

            def gated(s, half):
                dve.wait_ge(q_read, s * 4 + (2 * half + 2))
                dve.wait_ge(silu_ready, s * 2 + (half + 1))
                nc.vector.tensor_tensor(hidden[half][:, :], gate[:, :], act_up[:, :], ALU.mult).then_inc(h_ready, 1)

            def hidden_low(s, half):
                dve.wait_ge(hid_hi_ready, s * 2 + (half + 1))
                cols = slice(half * N, (half + 1) * N)
                subtract(hid_lo[:, cols], t_ps[half][:, :], hid_hi[:, cols]).then_inc(hid_lo_ready, 1)

            def finish(s, n):
                dve.wait_ge(stored[n], (s - n) * 8 + 16)
                dve.wait_ge(resid_ready, s + 1)
                dve.wait_ge(down_used, s * DN + DN)
                nc.vector.tensor_tensor(result[n][:, :], d_ps[:, :], resid[:, :], ALU.add).then_inc(result_ready, 1)

            def residual(s, run):
                dve.wait_ge(r_done, s + 1)
                nc.vector.tensor_tensor(resid[:, :], r_ps[:, :], bias[:, bass.ds((run % 2) * BIAS + 4 * N, N)], ALU.add)\
                  .then_inc(resid_ready, 1)

            def low_parts(changed, index, chunks, ready, first_chunk, in_step):
                with dve.If(changed > 0):
                    run = entry(dve, T_RUN, index, E - 1)
                    for c in chunks:
                        dve.wait_ge(w_hi_ready, run * CHUNKS + (c + 1))
                        w_low(c, c % RING, ready)
                        if c > chunks[0]:
                            dve.wait_ge(ready, index * in_step + (c - first_chunk))
                            dve.sem_inc(raw_free, 1)
                    dve.wait_ge(ready, index * in_step + (chunks[-1] + 1 - first_chunk))
                    dve.sem_inc(raw_free, 1)
                with dve.Else():
                    dve.sem_inc(ready, len(chunks))

            def step(s, n, first=False, last=False):
                run = entry(dve, T_RUN, s, E - 1)
                changed = None if first else entry(dve, T_CHANGED, s, 1)
                changes = None if last else entry(dve, T_CHANGED, s + 1, 1)
                if not first:
                    hidden_low(s - 1, 1)
                add_bias(s, 0, pre, run, wait_bias=True)
                if not first:
                    dve.wait_ge(h_ready, s * 2)
                add_bias(s, 1, gate, run)
                gated(s, 0)
                if not first:
                    finish(s - 1, 1 - n)
                if not first:
                    dve.wait_ge(result_ready, s)
                residual(s, run)
                if not first:
                    low_parts(changed, s, range(UG, CHUNKS), down_ready, UG, DN)
                add_bias(s, 2, pre, run)
                if not last:
                    low_parts(changes, s + 1, range(0, 2), ug_ready, 0, UG)
                hidden_low(s, 0)
                if not last:
                    low_parts(changes, s + 1, range(2, 4), ug_ready, 0, UG)
                    dve.wait_ge(x1_hi_ready, s + 2)
                    subtract(x1_split[1 - n][:, D:2 * D], x1[1 - n][:, :], x1_split[1 - n][:, 0:D]).then_inc(x1_lo_ready, 1)
                dve.wait_ge(h_ready, s * 2 + 1)
                add_bias(s, 3, gate, run)
                gated(s, 1)
                if not last:
                    low_parts(changes, s + 1, range(4, UG), ug_ready, 0, UG)

            dve.wait_ge(x1_hi_ready, 1)
            subtract(x1_split[0][:, D:2 * D], x1[0][:, :], x1_split[0][:, 0:D]).then_inc(x1_lo_ready, 1)
            step(0, 0, first=True)
            step(1, 1)
            with dve.Fori(1, B // 2 - 1) as i:
                step(i * 2, 0)
                step(i * 2 + 1, 1)
            step(B - 2, 0)
            step(B - 1, 1, last=True)
            hidden_low(B - 1, 1)
            finish(B - 1, 1)

        @block.tensor
        def _(pe):
            def product(dst, still_hi, still_lo, moving_hi, moving_lo, first, last):
                nc.tensor.matmul(dst, still_hi, moving_hi, start=first, stop=False)
                nc.tensor.matmul(dst, still_hi, moving_lo, start=False, stop=False)
                return nc.tensor.matmul(dst, still_lo, moving_hi, start=False, stop=last)

            def group(g, n, first=False):
                for k in range(KD):
                    if first:
                        pe.wait_ge(l0_lo_ready, k + 1)
                    pe.wait_ge(x_lo_ready, g * KD + (k + 1))
                    x_parts = xk(x_hi, k), xk(x_lo, k)
                    a = slice(k * L0C, k * L0C + ER)
                    if k == 0 and not first:
                        pe.wait_ge(low_scaled, g)
                    got = product(low_ps[:, :].rearrange("p (s t) -> p s t", s=GS), l0_hi[:, a], l0_lo[:, a], *x_parts, k == 0, k == KD - 1)
                    if k == KD - 1:
                        got.then_inc(low_done, 1)
                    for m in range(KD):
                        if k == 0 and not first:
                            pe.wait_ge(x1_made, g * KD + (m + 1 - KD))
                        w = slice(k * L0C + ER + m * P, k * L0C + ER + (m + 1) * P)
                        got = product(q_ps[m][:, :].rearrange("p (s t) -> p s t", s=GS), l0_hi[:, w], l0_lo[:, w], *x_parts, k == 0, False)
                    got.then_inc(x_used, 1)
                if first:
                    pe.wait_ge(l0_lo_ready, KD + 1)
                pe.wait_ge(low_lo_ready, g + 1)
                for m in range(KD):
                    w = slice(KD * L0C + m * P, KD * L0C + (m + 1) * P)
                    product(q_ps[m][:, :], l0_hi[:, w], l0_lo[:, w], low_hi[:, :], low_lo[:, :], False, True).then_inc(base_done, 1)

            group(0, 0, first=True)
            with pe.Fori(1, G) as g:
                group(g, None)

            def quarter(s, n, q, reused):
                if q == 0:
                    pe.wait_ge(x1_lo_ready, s + 1)
                if reused:
                    pe.wait_ge(q_read, s * 4 + (q - 3))
                for c in range(2 * q, 2 * q + 2):
                    pe.wait_ge(ug_ready, s * UG + (c + 1))
                    for k in range(2 * (c % 2), 2 * (c % 2) + 2):
                        f = slice(k * P, (k + 1) * P)
                        fl = slice(D + k * P, D + (k + 1) * P)
                        w = slice((4 * q + k) * N, (4 * q + k + 1) * N)
                        got = product(q_ps[q][:, :], x1_split[n][:, f], x1_split[n][:, fl], w_hi[:, w], w_lo[:, w], k == 0, k == KD - 1)
                    got.then_inc(ug_used, 1)

            def transpose(dst, src, blocks):
                for k in range(blocks):
                    got = nc.tensor.transpose(dst[:, k * P:(k + 1) * P], src[:, k * P:(k + 1) * P], ident[:, :])
                return got

            def transpose_hidden(s, half, reused):
                pe.wait_ge(h_ready, s * 2 + (half + 1))
                if reused:
                    pe.wait_ge(hid_lo_ready, s * 2 + (half - 1))
                transpose(t_ps[half], hidden[half], KD).then_inc(t_done, 1)

            def down(s, reused):
                if reused:
                    pe.wait_ge(result_ready, s)
                for c in range(DN):
                    pe.wait_ge(down_ready, s * DN + (c + 1))
                    if c % 2 == 0:
                        pe.wait_ge(hid_lo_ready, s * 2 + (c // 2 + 1))
                    for k in range(2 * c, 2 * c + 2):
                        f = slice(k * P, (k + 1) * P)
                        w = slice((2 * UG + k) * N, (2 * UG + k + 1) * N)
                        got = product(d_ps[:, :], hid_hi[:, f], hid_lo[:, f], w_hi[:, w], w_lo[:, w], k == 0, k == KH - 1)
                    got.then_inc(down_used, 1)

            def step(s, n, first=False, reused=True):
                quarter(s, n, 0, not first)
                if not first:
                    pe.wait_ge(resid_ready, s)
                transpose(r_ps, x1[n], KD).then_inc(r_done, 1)
                if not first:
                    transpose_hidden(s - 1, 1, reused)
                quarter(s, n, 1, not first)
                if not first:
                    down(s - 1, reused)
                quarter(s, n, 2, not first)
                transpose_hidden(s, 0, not first)
                quarter(s, n, 3, not first)

            pe.wait_ge(ident_ready, 2)
            step(0, 0, first=True)
            step(1, 1, reused=False)
            with pe.Fori(1, B // 2 - 1) as i:
                step(i * 2, 0)
                step(i * 2 + 1, 1)
            step(B - 2, 0)
            step(B - 1, 1)
            transpose_hidden(B - 1, 1, True)
            down(B - 1, True)


def kernel(x, cond_8, L0_cond_W_base, L0_cond_b_base, L0_cond_As, L0_cond_Bs, L1_cond_W_up, L1_cond_b_up,
           L1_cond_W_gate, L1_cond_b_gate, L1_cond_W_down, L1_cond_b_down):
    import numpy as np
    import concourse.bacc as bacc
    from concourse.bass_utils import run_bass_kernel_spmd

    x, cond = np.asarray(x), np.asarray(cond_8)
    x_t = x.reshape(G, GS, S, KD, P).transpose(0, 4, 1, 3, 2).reshape(G, P, GS * D)
    a_t = np.asarray(L0_cond_As).reshape(ER, KD, P).transpose(2, 1, 0)
    base_t = np.asarray(L0_cond_W_base).reshape(D, KD, P).transpose(2, 1, 0)
    b_t = np.asarray(L0_cond_Bs).transpose(0, 2, 1).reshape(ER, D)
    l0_w = np.concatenate([np.concatenate([a_t, base_t], axis=2).reshape(P, KD * L0C), b_t], axis=1)
    l0_b = np.asarray(L0_cond_b_base).reshape(KD, P).T

    def halves(w):
        return np.asarray(w).reshape(E, H // N, N, KD, P).transpose(0, 4, 1, 3, 2)

    up, gate = halves(L1_cond_W_up), halves(L1_cond_W_gate)
    down = np.asarray(L1_cond_W_down).reshape(E, D, KH, P).transpose(0, 3, 2, 1)
    parts = [up[:, :, 0], gate[:, :, 0], up[:, :, 1], gate[:, :, 1], down]
    l1_w = np.concatenate(parts, axis=2).reshape(E, P, BLOCKS * N)
    bu, bg, bd = np.asarray(L1_cond_b_up), np.asarray(L1_cond_b_gate), np.asarray(L1_cond_b_down)
    l1_b = np.concatenate([bu[:, :N], bg[:, :N], bu[:, N:], bg[:, N:], bd], axis=1)
    arrays = {
        "x_t": x_t, "cond_row": cond.reshape(1, B * E), "cond_t": np.repeat(cond.T, R, axis=0),
        "l0_w": l0_w, "l0_b": l0_b, "l1_w": l1_w, "l1_b": l1_b,
    }
    arrays = {name: np.ascontiguousarray(a) for name, a in arrays.items()}
    nc = bacc.Bacc("TRN2", target_bir_lowering=False, num_devices=1)
    args = [nc.dram_tensor(name, a.shape, mybir.dt.from_np(a.dtype), kind="ExternalInput").ap() for name, a in arrays.items()]
    out = nc.dram_tensor("out", (B, S, D), F32, kind="ExternalOutput").ap()
    program(nc, *args, out)
    result = run_bass_kernel_spmd(nc, [arrays], core_ids=[0])
    return result.results[0]["out"]
```

```python
from contextlib import ExitStack

import concourse.bass as bass
from concourse import mybir

F32 = mybir.dt.float32
F32R = mybir.dt.float32r
I32 = mybir.dt.int32
ACT = mybir.ActivationFunctionType
ALU = mybir.AluOpType
AX_X = mybir.AxisListType.X

P = 128
B, S, D = 32, 128, 512
E, H, R = 8, 1024, 16
KD = D // P
KH = H // P
N = 512
GS = N // S
G = B // GS
LORA_SCALE = 2.0

ER = E * R
L0C = ER + D
L0W = KD * L0C + D
BLOCKS = 2 * KD * (H // N) + KH
CH = 2 * N
CHUNKS = BLOCKS // 2
UG = 8
DN = CHUNKS - UG
RING = 6
XB = 3
BIAS = 5 * N

T_SAMPLE, T_WORD, T_EXPERT = 0, B, 2 * B
T_RUNS, T_LEN = 2 * B + E, 2 * B + 2 * E


def program(nc, x_t, cond_row, cond_t, l0_w, l0_b, l1_w, l1_b, out):
    assert ER == P and S == P and G == 8 and CHUNKS == 12
    x1_dram = nc.dram_tensor("x1_scratch", (B, P, KD * S), F32, kind="Internal").ap()

    with ExitStack() as ctx:
        at = [(nc.sbuf_base + 31) // 32 * 32]

        def place(name, cols, dt=F32, offset=None, parts=P):
            if offset is None:
                offset = at[0]
                at[0] += (4 * cols + 31) // 32 * 32
            return nc.alloc_sbuf_tensor_at(name, [parts, cols], dt, offset=offset)

        def sem(name):
            return ctx.enter_context(nc.semaphore(name))

        def over(tensor_at, name, sizes, dt=F32):
            made = []
            for n, cols in enumerate(sizes):
                made.append(place(f"{name}{n}", cols, dt, offset=tensor_at))
                tensor_at += 4 * cols
            return made

        w_hi = place("w_hi", BLOCKS * N, F32R)
        w_lo_at = at[0]
        w_lo = place("w_lo", BLOCKS * N, F32R)
        raw_at = at[0]
        raw = place("raw", RING * CH)
        bias_at = at[0]
        bias = place("bias", 2 * BIAS)
        ident = place("ident", P)
        lora_w = place("lora_w", B)
        base_b = place("base_b", KD)
        table = place("table", T_LEN, I32)
        l0_at = at[0]
        l0_hi = place("l0_hi", L0W, F32R)
        l0_lo = place("l0_lo", L0W, F32R)
        xg_at = at[0]
        xg = [place(f"xg{n}", GS * D) for n in range(2)]
        xg.append(place("xg2", GS * D, offset=bias_at + 4 * BIAS))
        xs_at = at[0]
        x_hi = place("x_hi", GS * D, F32R)
        x_lo = place("x_lo", GS * D, F32R)
        hs_at = at[0]
        low = place("low", N)
        low_hi = place("low_hi", N, F32R)
        low_lo = place("low_lo", N, F32R)
        assert at[0] <= nc.sbuf_usable_end, (at[0], nc.sbuf_usable_end)
        l0_raw = place("l0_raw", L0W, offset=w_lo_at + 4 * (BLOCKS * N - L0W))
        raw_late = place("raw_late", RING * CH, offset=l0_at)
        wide = [place(f"wide{n}", B * E, offset=raw_at + 4 * n * B * E, parts=1) for n in range(2)]
        rows = place("rows", 14 * B, parts=1)
        rows_i = place("rows_i", 4 * B, I32, parts=1)
        assert at[0] <= nc.sbuf_usable_end, (at[0], nc.sbuf_usable_end)
        x1_0, x1_1, pre, act_up = over(xg_at, "x1_", [D, D, N, N])
        x1 = [x1_0, x1_1]
        gate, hidden_0, resid = over(hs_at, "row_", [N, N, D])
        hidden_1, result_0, result_1 = over(xg_at + 4 * GS * D, "late_", [N, D, D])
        hidden, result = [hidden_0, hidden_1], [result_0, result_1]
        x1_split = over(xs_at, "x1_split", [2 * D, 2 * D], F32R)
        hid_hi, hid_lo = over(xs_at + 4 * 4 * D, "hid_split", [H, H], F32R)

        bank = [ctx.enter_context(nc.psum_tensor(f"bank{n}", [P, N], F32)) for n in range(8)]
        q_ps, t_ps, r_ps, d_ps = bank[0:4], bank[4:6], bank[6], bank[7]
        low_ps = bank[4]

        cond_loaded, lora_w_loaded, base_b_loaded = sem("cond_loaded"), sem("lora_w_loaded"), sem("base_b_loaded")
        l0_loaded = [sem(f"l0_loaded{n}") for n in range(KD + 1)]
        l0_hi_ready, l0_lo_ready = sem("l0_hi_ready"), sem("l0_lo_ready")
        iota_ready, ident_ready, table_step, table_ready = sem("iota_ready"), sem("ident_ready"), sem("table_step"), sem("table_ready")
        x_first = [sem(f"x_first{k}") for k in range(KD)]
        x_loaded = [sem(f"x_loaded{n}") for n in range(XB)]
        x_hi_ready, x_lo_ready, x_used = sem("x_hi_ready"), sem("x_lo_ready"), sem("x_used")
        low_done, low_scaled, low_hi_ready, low_lo_ready = sem("low_done"), sem("low_scaled"), sem("low_hi_ready"), sem("low_lo_ready")
        base_done, x1_made = sem("base_done"), sem("x1_made")
        x1_stored = [sem(f"x1_stored{n}") for n in range(XB)]
        raw_loaded = [sem(f"raw_loaded{n}") for n in range(CHUNKS)]
        bias_loaded = sem("bias_loaded")
        w_hi_ready, raw_free = sem("w_hi_ready"), sem("raw_free")
        w_ready, ug_used, down_used = sem("w_ready"), sem("ug_used"), sem("down_used")
        x1_loaded = [sem(f"x1_loaded{n}") for n in range(2)]
        x1_hi_ready, x1_lo_ready = sem("x1_hi_ready"), sem("x1_lo_ready")
        q_read, silu_ready, h_ready = sem("q_read"), sem("silu_ready"), sem("h_ready")
        t_done, hid_hi_ready, hid_lo_ready = sem("t_done"), sem("hid_hi_ready"), sem("hid_lo_ready")
        r_done, resid_ready, result_ready = sem("r_done"), sem("resid_ready"), sem("result_ready")
        stored = [sem(f"stored{n}") for n in range(2)]

        block = ctx.enter_context(nc.Block())

        def l0_piece(n):
            return slice(n * L0C, min((n + 1) * L0C, L0W))

        def xk(buf, k):
            return buf[:, :].rearrange("p (s k t) -> p s k t", s=GS, k=KD)[:, :, k, :]

        def chunk(buf, c):
            return buf[:, c * CH:(c + 1) * CH]

        def raw_chunk(c):
            return chunk(raw, c) if c < RING else chunk(raw_late, c - RING)

        def entry(eng, column, index, high):
            return eng.value_load(table[0:1, bass.ds(index + column, 1)], min_val=0, max_val=high)

        @block.sync
        def _(sp):
            sp.dma_start(l0_raw[:, l0_piece(0)], l0_w[:, l0_piece(0)]).then_inc(l0_loaded[0], 16)
            for k in range(KD):
                sp.dma_start(xk(xg[0], k), xk(x_t[0], k)).then_inc(x_first[k], 16)
                sp.dma_start(l0_raw[:, l0_piece(k + 1)], l0_w[:, l0_piece(k + 1)]).then_inc(l0_loaded[k + 1], 16)
            for n in range(1, XB):
                sp.dma_start(xg[n][:, :], x_t[n]).then_inc(x_loaded[n], 16)

            def load_chunk(run_expert, c, slot, into):
                sp.dma_start(into,
                             l1_w[bass.ds(run_expert, 1), :, c * CH:(c + 1) * CH].rearrange("a p n -> p (a n)"))\
                  .then_inc(raw_loaded[slot], 16)

            def load_bias(run_expert, offset):
                row = l1_b[bass.ds(run_expert, 1), :].to_broadcast([P, BIAS])
                sp.dma_start(bias[:, bass.ds(offset, BIAS)], row).then_inc(bias_loaded, 16)

            def load_x(g, n, stores):
                sp.wait_ge(x1_stored[n], 16 * stores)
                sp.dma_start(xg[n][:, :], x_t[g]).then_inc(x_loaded[n], 16)

            sp.wait_ge(table_ready, 1)
            first = entry(sp, T_EXPERT, 0, E - 1)
            for c in range(RING):
                load_chunk(first, c, c, chunk(raw, c))
            load_x(3, 0, 1)
            load_bias(first, 0)
            load_x(4, 1, 1)
            for c in range(RING, CHUNKS):
                sp.wait_ge(raw_free, c - RING + 1)
                load_chunk(first, c, c - RING, chunk(raw, c - RING))
                if c % 2 and c < CHUNKS - 1:
                    g = 5 + (c - RING) // 2
                    load_x(g, g % XB, g // XB)
            load_x(G - 1, (G - 1) % XB, (G - 1) // XB)
            runs = entry(sp, T_RUNS, 0, E)
            with sp.If(runs > 1):
                expert = entry(sp, T_EXPERT, 1, E - 1)
                sp.wait_ge(raw_free, CHUNKS)
                for c in range(RING):
                    load_chunk(expert, c, c, raw_chunk(c))
                sp.wait_ge(base_done, G * KD)
                for c in range(RING, CHUNKS):
                    load_chunk(expert, c, c, raw_chunk(c))
                sp.wait_ge(x1_stored[2], 16 * 2)
                sp.wait_ge(bias_loaded, 16)
                load_bias(expert, BIAS)
            with sp.Fori(2, E) as r:
                with sp.If(runs > r):
                    expert = entry(sp, T_EXPERT, r, E - 1)
                    for c in range(CHUNKS):
                        sp.wait_ge(raw_free, (r - 1) * CHUNKS + (c + 1))
                        load_chunk(expert, c, c, raw_chunk(c))
                    sp.wait_ge(bias_loaded, r * 16)
                    load_bias(expert, (r % 2) * BIAS)

        @block.gpsimd
        def _(pool):
            nc.gpsimd.iota(rows_i[0:1, 0:E], pattern=[[-1, E]], base=E, channel_multiplier=0).then_inc(iota_ready, 1)
            nc.gpsimd.iota(rows_i[0:1, B:2 * B], pattern=[[1, B]], base=0, channel_multiplier=0).then_inc(iota_ready, 1)
            nc.gpsimd.memset(ident[:, :], 0.0).then_inc(ident_ready, 1)
            pool.wait_ge(ident_ready, 1)
            nc.gpsimd.affine_select(out=ident[:, :], in_=ident[:, :], compare_op=ALU.not_equal, fill=1.0, base=0,
                                    pattern=[[-1, P]], channel_multiplier=1).then_inc(ident_ready, 1)

        @block.scalar
        def _(act):
            act.dma_start(rows[0:1, 0:B * E], cond_row).then_inc(cond_loaded, 16)
            act.dma_start(lora_w[:, :], cond_t).then_inc(lora_w_loaded, 16)
            act.dma_start(base_b[:, :], l0_b).then_inc(base_b_loaded, 16)

            def x_high(g, n, k):
                nc.scalar.activation(xk(x_hi, k), xk(xg[n], k), ACT.Copy).then_inc(x_hi_ready, 1)

            def l0_high(n):
                act.wait_ge(l0_loaded[n], 16)
                nc.scalar.activation(l0_hi[:, l0_piece(n)], l0_raw[:, l0_piece(n)], ACT.Copy).then_inc(l0_hi_ready, 1)

            def next_x_high(g, n, k):
                act.wait_ge(x_used, (g - 1) * KD + (k + 1))
                x_high(g, n, k)

            def first_run_high(i, n):
                act.wait_ge(raw_loaded[n], i * 16 + 16)
                nc.scalar.activation(w_hi[:, bass.ds(i * (RING * CH) + n * CH, CH)], chunk(raw, n), ACT.Copy)\
                  .then_inc(w_hi_ready, 1)

            def low_high(g):
                act.wait_ge(low_scaled, g + 1)
                nc.scalar.activation(low_hi[:, :], low[:, :], ACT.Copy).then_inc(low_hi_ready, 1)

            def store_x1(g, n):
                act.wait_ge(x1_made, g * KD + KD)
                act.dma_start(x1_dram[bass.ds(g * GS, GS)].rearrange("s p n -> p s n"),
                              xg[n][:, :].rearrange("p (s n) -> p s n", s=GS)).then_inc(x1_stored[n], 16)

            def group(g, n, loaded, weights=None):
                for k in range(KD - 1):
                    if k == 0:
                        act.wait_ge(x_loaded[(n + 1) % XB], loaded)
                    next_x_high(g + 1, (n + 1) % XB, k)
                    if weights is not None and k < 2:
                        first_run_high(weights[0], weights[1] + k)
                low_high(g)
                next_x_high(g + 1, (n + 1) % XB, KD - 1)
                store_x1(g, n)

            for k in range(KD):
                l0_high(k)
                act.wait_ge(x_first[k], 16)
                x_high(0, 0, k)
            l0_high(KD)
            group(0, 0, 16)
            with act.Fori(0, (G - 2) // XB) as i:
                for n in range(XB):
                    group(i * XB + (n + 1), (n + 1) % XB, i * 16 + (32 if n == 2 else 16), weights=(i, 2 * n))
            low_high(G - 1)

            act.sem_inc(stored[0], 16)
            act.sem_inc(stored[1], 16)

            def load_x1(s, n):
                sample = entry(act, T_SAMPLE, s, B - 1)
                act.dma_start(x1[n][:, :], x1_dram[bass.ds(sample, 1)].rearrange("a p n -> p (a n)")).then_inc(x1_loaded[n], 16)

            def x1_high(s, n, used=True):
                act.wait_ge(x1_loaded[n], (s - n) * 8 + 16)
                if used:
                    act.wait_ge(ug_used, (s - 1) * UG)
                nc.scalar.activation(x1_split[n][:, 0:D], x1[n][:, :], ACT.Copy).then_inc(x1_hi_ready, 1)

            def hidden_high(s, half):
                act.wait_ge(t_done, s * 2 + (half + 1))
                cols = slice(half * N, (half + 1) * N)
                nc.scalar.activation(hid_hi[:, cols], t_ps[half][:, :], ACT.Copy).then_inc(hid_hi_ready, 1)

            def silu(s, half, free):
                act.wait_ge(q_read, s * 4 + (2 * half + 1))
                if free:
                    act.wait_ge(h_ready, s * 2 + half)
                nc.scalar.activation(act_up[:, :], pre[:, :], ACT.Silu).then_inc(silu_ready, 1)

            def store(s, n):
                sample = entry(act, T_SAMPLE, s, B - 1)
                act.wait_ge(result_ready, s + 1)
                act.dma_start(out[bass.ds(sample, 1)].rearrange("a t d -> t (a d)"), result[n][:, :]).then_inc(stored[n], 16)

            def high_parts(changed, runs_before, index, chunks):
                with act.If(changed > 0):
                    for c in chunks:
                        act.wait_ge(raw_loaded[c], runs_before * 16 + (48 if c < RING else 16))
                        if c < UG:
                            act.wait_ge(ug_used, (index - 1) * UG + (c + 1))
                        else:
                            act.wait_ge(down_used, (index - 1) * DN + (c + 1 - UG))
                        nc.scalar.activation(chunk(w_hi, c), raw_chunk(c), ACT.Copy).then_inc(w_hi_ready, 1)

            def step(s, n, first=False, last=False, ahead_ends=False):
                if not first:
                    hidden_high(s - 1, 1)
                silu(s, 0, not first)
                if first:
                    for m, stores in enumerate((3, 3, 2)):
                        act.wait_ge(x1_stored[m], 16 * stores)
                    load_x1(1, 1)
                if not last:
                    x1_high(s + 1, 1 - n, used=not first)
                if not ahead_ends:
                    act.wait_ge(r_done, s + 1)
                    load_x1(s + 2, n)
                word = entry(act, T_WORD, s, 255)
                if not first:
                    last_run = entry(act, T_WORD, s - 1, 255) // 16
                    high_parts(word % 2, last_run, s, range(UG, CHUNKS))
                if not last:
                    high_parts(word // 4 % 2, word // 16, s + 1, range(0, 4))
                if not first:
                    store(s - 1, 1 - n)
                silu(s, 1, True)
                hidden_high(s, 0)
                if not last:
                    high_parts(word // 8 % 2, word // 16, s + 1, range(0, 4))
                    high_parts(word // 2 % 2, word // 16, s + 1, range(4, UG))

            act.wait_ge(x1_stored[0], 16 * 3)
            load_x1(0, 0)
            act.wait_ge(x_used, G * KD)
            x1_high(0, 0, used=False)
            store_x1(G - 1, 1)
            step(0, 0, first=True)
            step(1, 1)
            with act.Fori(1, B // 2 - 1) as i:
                step(i * 2, 0)
                step(i * 2 + 1, 1)
            step(B - 2, 0, ahead_ends=True)
            step(B - 1, 1, last=True, ahead_ends=True)
            hidden_high(B - 1, 1)
            store(B - 1, 1)
            act.wait_ge(stored[0], 16 + 16 * B // 2)
            act.wait_ge(stored[1], 16 + 16 * B // 2)

        @block.vector
        def _(dve):
            done = [0]

            def then(instruction):
                done[0] += 1
                instruction.then_inc(table_step, 1)
                dve.wait_ge(table_step, done[0])

            def row(n):
                return rows[0:1, (8 + n) * B:(9 + n) * B]

            def square(buf, a=B, b=B):
                return buf[0:1, 0:a * b].rearrange("p (a b) -> p a b", a=a)

            def outer(r, a=B, b=B):
                return r.unsqueeze(2).to_broadcast([1, a, b])

            def inner(r, a=B, b=B):
                return r.unsqueeze(1).to_broadcast([1, a, b])

            spare, ordered, index, down8 = row(0), row(2), row(3), row(4)[:, 0:E]
            first8 = row(4)[:, E:E + 1]

            def sort_samples():
                key, other = row(1), rows[0:1, 13 * B:14 * B]
                dve.wait_ge(iota_ready, 2)
                dve.wait_ge(cond_loaded, 16)
                then(nc.vector.tensor_copy(down8, rows_i[0:1, 0:E]))
                then(nc.vector.tensor_copy(index, rows_i[0:1, B:2 * B]))
                cond3 = rows[0:1, 0:B * E].rearrange("p (b e) -> p b e", b=B)
                then(nc.vector.tensor_reduce(spare, cond3, AX_X, ALU.max))
                then(nc.vector.tensor_tensor(square(wide[0], B, E), cond3, outer(spare, B, E), ALU.is_ge))
                then(nc.vector.tensor_tensor(square(wide[1], B, E), square(wide[0], B, E), inner(down8, B, E), ALU.mult))
                then(nc.vector.tensor_reduce(spare, square(wide[1], B, E), AX_X, ALU.max))
                then(nc.vector.tensor_scalar(spare, spare, 1.0, None, ALU.max))
                then(nc.vector.tensor_copy(first8, spare[:, 0:1]))
                then(nc.vector.tensor_tensor(spare, spare, first8.to_broadcast([1, B]), ALU.subtract))
                then(nc.vector.tensor_scalar(other, spare, 0.0, -float(B * E), ALU.is_gt, ALU.mult))
                then(nc.vector.scalar_tensor_tensor(key, spare, float(B), other, ALU.mult, ALU.add))
                then(nc.vector.tensor_tensor(key, key, index, ALU.subtract))
                for n in range(B // 8):
                    top = ordered[:, 8 * n:8 * n + 8]
                    then(nc.vector.max(top, key))
                    then(nc.vector.match_replace(other, top, key, -1e9))
                    key, other = other, key
                then(nc.vector.tensor_scalar(spare, ordered, -1.0, None, ALU.mult))
                keys_i, behind_i = rows_i[0:1, 2 * B:3 * B], rows_i[0:1, 3 * B:4 * B]
                then(nc.vector.tensor_copy(keys_i, spare))
                then(nc.vector.tensor_single_scalar(table[0:1, T_SAMPLE:T_SAMPLE + B], keys_i, B - 1, ALU.bitwise_and))
                then(nc.vector.tensor_single_scalar(behind_i, keys_i, 5, ALU.arith_shift_right))
                behind, changed, run, shifted, after = ordered, key, other, spare, rows[0:1, 0:B]
                then(nc.vector.tensor_copy(behind, behind_i))
                then(nc.vector.memset(changed, 0.0))
                then(nc.vector.tensor_tensor(changed[:, 1:B], behind[:, 1:B], behind[:, 0:B - 1], ALU.not_equal))
                then(nc.vector.tensor_copy(run, changed))
                for n in range(5):
                    by = 2 ** n
                    then(nc.vector.tensor_copy(shifted, run))
                    then(nc.vector.tensor_tensor(run[:, by:B], shifted[:, by:B], shifted[:, 0:B - by], ALU.add))
                then(nc.vector.memset(after, 0.0))
                then(nc.vector.tensor_copy(after[:, 0:B - 1], changed[:, 1:B]))
                then(nc.vector.scalar_tensor_tensor(shifted, run, 16.0, changed, ALU.mult, ALU.add))
                then(nc.vector.tensor_tensor(changed, changed, after, ALU.mult))
                then(nc.vector.scalar_tensor_tensor(shifted, after, 6.0, shifted, ALU.mult, ALU.add))
                then(nc.vector.scalar_tensor_tensor(shifted, changed, 4.0, shifted, ALU.mult, ALU.add))
                then(nc.vector.tensor_copy(table[0:1, T_WORD:T_WORD + B], shifted))
                then(nc.vector.tensor_scalar(table[0:1, T_RUNS:T_RUNS + 1], run[:, B - 1:B], 1.0, None, ALU.add))
                of_run = after[:, 0:E]
                then(nc.vector.tensor_tensor(square(wide[0], E, B), outer(index[:, 0:E], E, B), inner(run, E, B), ALU.is_equal))
                then(nc.vector.tensor_tensor(square(wide[1], E, B), square(wide[0], E, B), inner(behind, E, B), ALU.mult))
                then(nc.vector.tensor_reduce(of_run, square(wide[1], E, B), AX_X, ALU.max))
                then(nc.vector.tensor_tensor(of_run, of_run, first8.to_broadcast([1, E]), ALU.subtract))
                then(nc.vector.tensor_scalar(of_run, of_run, float(E), None, ALU.add))
                then(nc.vector.tensor_copy(keys_i[:, 0:E], of_run))
                nc.vector.tensor_single_scalar(table[0:1, T_EXPERT:T_EXPERT + E], keys_i[:, 0:E], E - 1, ALU.bitwise_and)\
                  .then_inc(table_ready, 1)

            def subtract(lo, whole, hi):
                return nc.vector.tensor_tensor(lo, whole, hi.bitcast(F32), ALU.subtract)

            def l0_low(n):
                dve.wait_ge(l0_hi_ready, n + 1)
                subtract(l0_lo[:, l0_piece(n)], l0_raw[:, l0_piece(n)], l0_hi[:, l0_piece(n)]).then_inc(l0_lo_ready, 1)

            def x_low(g, n, k):
                dve.wait_ge(x_hi_ready, g * KD + (k + 1))
                subtract(xk(x_lo, k), xk(xg[n], k), xk(x_hi, k)).then_inc(x_lo_ready, 1)

            def w_low(c, whole):
                at_c = bass.ds(c * CH, CH)
                subtract(w_lo[:, at_c], whole, w_hi[:, at_c]).then_inc(w_ready, 1)

            def first_run_low(i, n):
                dve.wait_ge(w_hi_ready, i * RING + (n + 1))
                w_low(i * RING + n, chunk(raw, n))
                dve.wait_ge(w_ready, i * RING + (n + 1))
                dve.sem_inc(raw_free, 1)

            def x1_low(s, n):
                dve.wait_ge(x1_hi_ready, s + 1)
                subtract(x1_split[n][:, D:2 * D], x1[n][:, :], x1_split[n][:, 0:D]).then_inc(x1_lo_ready, 1)

            def group(g, n, weights=None, first=False, last=False):
                if first:
                    sort_samples()
                if not last:
                    for k in range(KD - 1):
                        if not first:
                            x_low(g + 1, (n + 1) % XB, k)
                        if weights is not None and k < 2:
                            first_run_low(weights[0], weights[1] + k)
                dve.wait_ge(low_done, g + 1)
                if not first:
                    dve.wait_ge(low_lo_ready, g)
                nc.vector.tensor_tensor(low[:, :].rearrange("p (s t) -> p s t", s=GS),
                                        low_ps[:, :].rearrange("p (s t) -> p s t", s=GS),
                                        lora_w[:, bass.ds(g * GS, GS)].unsqueeze(2).to_broadcast([P, GS, S]),
                                        ALU.mult).then_inc(low_scaled, 1)
                dve.wait_ge(low_hi_ready, g + 1)
                subtract(low_lo[:, :], low[:, :], low_hi[:, :]).then_inc(low_lo_ready, 1)
                if not last:
                    for k in range(KD):
                        if first or k == KD - 1:
                            x_low(g + 1, (n + 1) % XB, k)
                else:
                    x1_low(0, 0)
                for m in range(KD):
                    dve.wait_ge(base_done, g * KD + (m + 1))
                    nc.vector.scalar_tensor_tensor(xk(xg[n], m), q_ps[m][:, :].rearrange("p (s t) -> p s t", s=GS),
                                                   base_b[:, m:m + 1], xk(xg[n], m), ALU.add, ALU.add)\
                      .then_inc(x1_made, 1)

            for k in range(KD):
                l0_low(k)
                x_low(0, 0, k)
            l0_low(KD)
            dve.wait_ge(lora_w_loaded, 16)
            nc.vector.tensor_scalar(lora_w[:, :], lora_w[:, :], LORA_SCALE, None, ALU.mult).then_inc(lora_w_loaded, 1)
            dve.wait_ge(lora_w_loaded, 17)
            dve.wait_ge(base_b_loaded, 16)
            group(0, 0, first=True)
            with dve.Fori(0, (G - 2) // XB) as i:
                for n in range(XB):
                    group(i * XB + (n + 1), (n + 1) % XB, weights=(i, 2 * n))
            group(G - 1, 1, last=True)

            def add_bias(s, q, dst, run, wait_bias=False):
                if wait_bias:
                    dve.wait_ge(bias_loaded, run * 16 + 16)
                dve.wait_ge(ug_used, s * UG + (2 * q + 2))
                nc.vector.tensor_tensor(dst[:, :], q_ps[q][:, :], bias[:, bass.ds((run % 2) * BIAS + q * N, N)], ALU.add)\
                  .then_inc(q_read, 1)

            def gated(s, half):
                dve.wait_ge(q_read, s * 4 + (2 * half + 2))
                dve.wait_ge(silu_ready, s * 2 + (half + 1))
                nc.vector.tensor_tensor(hidden[half][:, :], gate[:, :], act_up[:, :], ALU.mult).then_inc(h_ready, 1)

            def hidden_low(s, half):
                dve.wait_ge(hid_hi_ready, s * 2 + (half + 1))
                cols = slice(half * N, (half + 1) * N)
                subtract(hid_lo[:, cols], t_ps[half][:, :], hid_hi[:, cols]).then_inc(hid_lo_ready, 1)

            def finish(s, n):
                dve.wait_ge(stored[n], (s - n) * 8 + 16)
                dve.wait_ge(resid_ready, s + 1)
                dve.wait_ge(down_used, s * DN + DN)
                nc.vector.tensor_tensor(result[n][:, :], d_ps[:, :], resid[:, :], ALU.add).then_inc(result_ready, 1)

            def residual(s, run):
                dve.wait_ge(r_done, s + 1)
                nc.vector.tensor_tensor(resid[:, :], r_ps[:, :], bias[:, bass.ds((run % 2) * BIAS + 4 * N, N)], ALU.add)\
                  .then_inc(resid_ready, 1)

            def low_parts(run, index, chunks):
                for c in chunks:
                    dve.wait_ge(w_hi_ready, run * CHUNKS + (c + 1))
                    w_low(c, raw_chunk(c))
                    if c > chunks[0]:
                        dve.wait_ge(w_ready, index * CHUNKS + c)
                        dve.sem_inc(raw_free, 1)
                dve.wait_ge(w_ready, index * CHUNKS + (chunks[-1] + 1))
                dve.sem_inc(raw_free, 1)

            def step(s, n, first=False, last=False):
                if not first:
                    hidden_low(s - 1, 1)
                word = entry(dve, T_WORD, s, 255)
                run = dve.snap(word // 16)
                add_bias(s, 0, pre, run, wait_bias=True)
                if not first:
                    dve.wait_ge(h_ready, s * 2)
                add_bias(s, 1, gate, run)
                gated(s, 0)
                if not last:
                    x1_low(s + 1, 1 - n)
                if not first:
                    with dve.If(word % 2 > 0):
                        low_parts(run, s, range(UG, CHUNKS))
                    with dve.Else():
                        dve.sem_inc(w_ready, DN)
                if not last:
                    with dve.If(word // 2 % 2 > 0):
                        with dve.If(word // 4 % 2 > 0):
                            low_parts(run + 1, s + 1, range(0, 4))
                    with dve.Else():
                        dve.sem_inc(w_ready, UG)
                if not first:
                    finish(s - 1, 1 - n)
                    dve.wait_ge(result_ready, s)
                residual(s, run)
                add_bias(s, 2, pre, run)
                hidden_low(s, 0)

                def last_quarter():
                    dve.wait_ge(h_ready, s * 2 + 1)
                    add_bias(s, 3, gate, run)
                    gated(s, 1)

                if last:
                    last_quarter()
                else:
                    with dve.If(word // 2 % 2 > 0):
                        with dve.If(word // 8 % 2 > 0):
                            low_parts(run + 1, s + 1, range(0, 4))
                        last_quarter()
                        low_parts(run + 1, s + 1, range(4, UG))
                    with dve.Else():
                        last_quarter()

            step(0, 0, first=True)
            step(1, 1)
            with dve.Fori(1, B // 2 - 1) as i:
                step(i * 2, 0)
                step(i * 2 + 1, 1)
            step(B - 2, 0)
            step(B - 1, 1, last=True)
            hidden_low(B - 1, 1)
            finish(B - 1, 1)

        @block.tensor
        def _(pe):
            def product(dst, still_hi, still_lo, moving_hi, moving_lo, first, last):
                nc.tensor.matmul(dst, still_hi, moving_hi, start=first, stop=False)
                nc.tensor.matmul(dst, still_hi, moving_lo, start=False, stop=False)
                return nc.tensor.matmul(dst, still_lo, moving_hi, start=False, stop=last)

            def group(g, n, first=False):
                for k in range(KD):
                    if first:
                        pe.wait_ge(l0_lo_ready, k + 1)
                    pe.wait_ge(x_lo_ready, g * KD + (k + 1))
                    x_parts = xk(x_hi, k), xk(x_lo, k)
                    a = slice(k * L0C, k * L0C + ER)
                    if k == 0 and not first:
                        pe.wait_ge(low_scaled, g)
                    got = product(low_ps[:, :].rearrange("p (s t) -> p s t", s=GS), l0_hi[:, a], l0_lo[:, a], *x_parts, k == 0, k == KD - 1)
                    if k == KD - 1:
                        got.then_inc(low_done, 1)
                    for m in range(KD):
                        if k == 0 and not first:
                            pe.wait_ge(x1_made, g * KD + (m + 1 - KD))
                        w = slice(k * L0C + ER + m * P, k * L0C + ER + (m + 1) * P)
                        got = product(q_ps[m][:, :].rearrange("p (s t) -> p s t", s=GS), l0_hi[:, w], l0_lo[:, w], *x_parts, k == 0, False)
                    got.then_inc(x_used, 1)
                if first:
                    pe.wait_ge(l0_lo_ready, KD + 1)
                pe.wait_ge(low_lo_ready, g + 1)
                for m in range(KD):
                    w = slice(KD * L0C + m * P, KD * L0C + (m + 1) * P)
                    product(q_ps[m][:, :], l0_hi[:, w], l0_lo[:, w], low_hi[:, :], low_lo[:, :], False, True).then_inc(base_done, 1)

            group(0, 0, first=True)
            with pe.Fori(1, G) as g:
                group(g, None)

            def quarter(s, n, q, reused):
                if q == 0:
                    pe.wait_ge(x1_lo_ready, s + 1)
                if reused:
                    pe.wait_ge(q_read, s * 4 + (q - 3))
                else:
                    pe.wait_ge(x1_made, (G - 1) * KD + (q + 1))
                for c in range(2 * q, 2 * q + 2):
                    pe.wait_ge(w_ready, s * CHUNKS + (c + 1))
                    for k in range(2 * (c % 2), 2 * (c % 2) + 2):
                        f = slice(k * P, (k + 1) * P)
                        fl = slice(D + k * P, D + (k + 1) * P)
                        w = slice((4 * q + k) * N, (4 * q + k + 1) * N)
                        got = product(q_ps[q][:, :], x1_split[n][:, f], x1_split[n][:, fl], w_hi[:, w], w_lo[:, w], k == 0, k == KD - 1)
                    got.then_inc(ug_used, 1)

            def transpose(dst, src, blocks):
                for k in range(blocks):
                    got = nc.tensor.transpose(dst[:, k * P:(k + 1) * P], src[:, k * P:(k + 1) * P], ident[:, :])
                return got

            def transpose_hidden(s, half, reused):
                pe.wait_ge(h_ready, s * 2 + (half + 1))
                if reused:
                    pe.wait_ge(hid_lo_ready, s * 2 + (half - 1))
                transpose(t_ps[half], hidden[half], KD).then_inc(t_done, 1)

            def down(s, reused):
                if reused:
                    pe.wait_ge(result_ready, s)
                for c in range(DN):
                    pe.wait_ge(w_ready, s * CHUNKS + (UG + c + 1))
                    if c % 2 == 0:
                        pe.wait_ge(hid_lo_ready, s * 2 + (c // 2 + 1))
                    for k in range(2 * c, 2 * c + 2):
                        f = slice(k * P, (k + 1) * P)
                        w = slice((2 * UG + k) * N, (2 * UG + k + 1) * N)
                        got = product(d_ps[:, :], hid_hi[:, f], hid_lo[:, f], w_hi[:, w], w_lo[:, w], k == 0, k == KH - 1)
                    got.then_inc(down_used, 1)

            def step(s, n, first=False, reused=True):
                quarter(s, n, 0, not first)
                if not first:
                    pe.wait_ge(resid_ready, s)
                transpose(r_ps, x1[n], KD).then_inc(r_done, 1)
                if not first:
                    transpose_hidden(s - 1, 1, reused)
                quarter(s, n, 1, not first)
                if not first:
                    down(s - 1, reused)
                quarter(s, n, 2, not first)
                transpose_hidden(s, 0, not first)
                quarter(s, n, 3, not first)

            pe.wait_ge(ident_ready, 2)
            step(0, 0, first=True)
            step(1, 1, reused=False)
            with pe.Fori(1, B // 2 - 1) as i:
                step(i * 2, 0)
                step(i * 2 + 1, 1)
            step(B - 2, 0)
            step(B - 1, 1)
            transpose_hidden(B - 1, 1, True)
            down(B - 1, True)


def kernel(x, cond_8, L0_cond_W_base, L0_cond_b_base, L0_cond_As, L0_cond_Bs, L1_cond_W_up, L1_cond_b_up,
           L1_cond_W_gate, L1_cond_b_gate, L1_cond_W_down, L1_cond_b_down):
    import numpy as np
    import concourse.bacc as bacc
    from concourse.bass_utils import run_bass_kernel_spmd

    x, cond = np.asarray(x), np.asarray(cond_8)
    x_t = x.reshape(G, GS, S, KD, P).transpose(0, 4, 1, 3, 2).reshape(G, P, GS * D)
    a_t = np.asarray(L0_cond_As).reshape(ER, KD, P).transpose(2, 1, 0)
    base_t = np.asarray(L0_cond_W_base).reshape(D, KD, P).transpose(2, 1, 0)
    b_t = np.asarray(L0_cond_Bs).transpose(0, 2, 1).reshape(ER, D)
    l0_w = np.concatenate([np.concatenate([a_t, base_t], axis=2).reshape(P, KD * L0C), b_t], axis=1)
    l0_b = np.asarray(L0_cond_b_base).reshape(KD, P).T

    def halves(w):
        return np.asarray(w).reshape(E, H // N, N, KD, P).transpose(0, 4, 1, 3, 2)

    up, gate = halves(L1_cond_W_up), halves(L1_cond_W_gate)
    down = np.asarray(L1_cond_W_down).reshape(E, D, KH, P).transpose(0, 3, 2, 1)
    parts = [up[:, :, 0], gate[:, :, 0], up[:, :, 1], gate[:, :, 1], down]
    l1_w = np.concatenate(parts, axis=2).reshape(E, P, BLOCKS * N)
    bu, bg, bd = np.asarray(L1_cond_b_up), np.asarray(L1_cond_b_gate), np.asarray(L1_cond_b_down)
    l1_b = np.concatenate([bu[:, :N], bg[:, :N], bu[:, N:], bg[:, N:], bd], axis=1)
    arrays = {
        "x_t": x_t, "cond_row": cond.reshape(1, B * E), "cond_t": np.repeat(cond.T, R, axis=0),
        "l0_w": l0_w, "l0_b": l0_b, "l1_w": l1_w, "l1_b": l1_b,
    }
    arrays = {name: np.ascontiguousarray(a) for name, a in arrays.items()}
    nc = bacc.Bacc("TRN2", target_bir_lowering=False, num_devices=1)
    args = [nc.dram_tensor(name, a.shape, mybir.dt.from_np(a.dtype), kind="ExternalInput").ap() for name, a in arrays.items()]
    out = nc.dram_tensor("out", (B, S, D), F32, kind="ExternalOutput").ap()
    program(nc, *args, out)
    result = run_bass_kernel_spmd(nc, [arrays], core_ids=[0])
    return result.results[0]["out"]
```

```python
from contextlib import ExitStack

import concourse.bass as bass
from concourse import mybir

F32 = mybir.dt.float32
F32R = mybir.dt.float32r
I32 = mybir.dt.int32
ACT = mybir.ActivationFunctionType
ALU = mybir.AluOpType
AX_X = mybir.AxisListType.X

P = 128
B, S, D = 32, 128, 512
E, H, R = 8, 1024, 16
KD = D // P
KH = H // P
N = 512
GS = N // S
G = B // GS
LORA_SCALE = 2.0

ER = E * R
L0C = ER + D
L0W = KD * L0C + D
BLOCKS = 2 * KD * (H // N) + KH
CH = 2 * N
CHUNKS = BLOCKS // 2
UG = 8
DN = CHUNKS - UG
DV = 5
PL = CHUNKS - DV
RING = 6
BIAS = 5 * N
XB = 3
WARM = 9
QUAD = 32
QUADS = (P // QUAD) ** 2

T_SAMPLE, T_WORD, T_EXPERT = 0, B, 2 * B
T_RUNS = T_EXPERT + E
T_LEN = T_RUNS + 1


def program(nc, x_t, cond_row, cond_t, l0_w, l0_b, l1_w, l1_b, out):
    assert ER == P and S == P and G == 8 and CHUNKS == 12
    x1_dram = nc.dram_tensor("x1_scratch", (B, P, KD * S), F32, kind="Internal").ap()

    with ExitStack() as ctx:
        at = [(nc.sbuf_base + 31) // 32 * 32]

        def place(name, cols, dt=F32, offset=None, parts=P):
            if offset is None:
                offset = at[0]
                at[0] += (4 * cols + 31) // 32 * 32
            return nc.alloc_sbuf_tensor_at(name, [parts, cols], dt, offset=offset)

        def sem(name):
            return ctx.enter_context(nc.semaphore(name))

        def over(tensor_at, name, sizes, dt=F32):
            made = []
            for n, cols in enumerate(sizes):
                made.append(place(f"{name}{n}", cols, dt, offset=tensor_at))
                tensor_at += 4 * cols
            return made

        w_hi = place("w_hi", BLOCKS * N, F32R)
        w_lo_at = at[0]
        w_lo = place("w_lo", BLOCKS * N, F32R)
        raw_at = at[0]
        raw = place("raw", RING * CH)
        bias_at = at[0]
        bias = place("bias", 2 * BIAS)
        ident = place("ident", P)
        lora_w = place("lora_w", B)
        base_b = place("base_b", KD)
        table = place("table", T_LEN, I32)
        one = place("one", 8)
        x1_0 = place("x1_0", D)
        l0_at = at[0]
        l0_hi = place("l0_hi", L0W, F32R)
        l0_lo = place("l0_lo", L0W, F32R)
        xg_at = at[0]
        xg = [place(f"xg{n}", GS * D) for n in range(2)]
        xg.append(place("xg2", GS * D, offset=bias_at + 4 * BIAS))
        xs_at = at[0]
        x_hi = place("x_hi", GS * D, F32R)
        x_lo = place("x_lo", GS * D, F32R)
        hs_at = at[0]
        low = place("low", N)
        low_hi = place("low_hi", N, F32R)
        low_lo = place("low_lo", N, F32R)
        assert at[0] <= nc.sbuf_usable_end, (at[0], nc.sbuf_usable_end)
        l0_raw = place("l0_raw", L0W, offset=w_lo_at + 4 * (BLOCKS * N - L0W))
        raw_late = place("raw_late", RING * CH, offset=l0_at)
        wide = [place(f"wide{n}", B * E, offset=raw_at + 4 * n * B * E, parts=1) for n in range(2)]
        cond = place("cond", B * E, parts=1)
        sort_rows = place("sort_rows", 6 * B, parts=1)
        sort_rows_i = place("sort_rows_i", 4 * B, I32, parts=1)
        assert at[0] <= nc.sbuf_usable_end, (at[0], nc.sbuf_usable_end)
        x1_1, pre, act_up = over(xg_at, "early_", [D, N, N])
        x1 = [x1_0, x1_1]
        gate, hidden_0, resid_0 = over(hs_at, "row_", [N, N, D])
        hidden_1, result_0, result_1, resid_1 = over(xg_at + 4 * GS * D, "late_", [N, D, D, D])
        resid = [resid_0, resid_1]
        hidden, result = [hidden_0, hidden_1], [result_0, result_1]
        x1_split = over(xs_at, "x1_split", [2 * D, 2 * D], F32R)
        hid_hi, hid_lo = over(xs_at + 4 * 4 * D, "hid_split", [H, H], F32R)

        bank = [ctx.enter_context(nc.psum_tensor(f"bank{n}", [P, N], F32)) for n in range(8)]
        q_ps, t_ps, d_ps, last_d_ps = bank[0:4], bank[4:6], bank[6], bank[7]
        low_ps = bank[4]

        cond_loaded, lora_w_loaded, base_b_loaded = sem("cond_loaded"), sem("lora_w_loaded"), sem("base_b_loaded")
        l0_loaded = [sem(f"l0_loaded{n}") for n in range(KD + 1)]
        l0_hi_ready, l0_lo_ready = sem("l0_hi_ready"), sem("l0_lo_ready")
        one_ready, one_used = sem("one_ready"), sem("one_used")
        iota_ready, ident_ready, table_step, table_ready = sem("iota_ready"), sem("ident_ready"), sem("table_step"), sem("table_ready")
        x_first = [sem(f"x_first{k}") for k in range(KD)]
        x_loaded = [sem(f"x_loaded{n}") for n in range(XB)]
        x_hi_ready, x_lo_ready, x_used = sem("x_hi_ready"), sem("x_lo_ready"), sem("x_used")
        low_done, low_scaled, low_hi_ready, low_lo_ready = sem("low_done"), sem("low_scaled"), sem("low_hi_ready"), sem("low_lo_ready")
        base_done, x1_made = sem("base_done"), sem("x1_made")
        x1_stored = [sem(f"x1_stored{n}") for n in range(XB)]
        raw_loaded = [sem(f"raw_loaded{n}") for n in range(CHUNKS)]
        bias_loaded = sem("bias_loaded")
        w_hi_ready, raw_free, late_free = sem("w_hi_ready"), sem("raw_free"), sem("late_free")
        w_ready, late_ready, ug_used, down_used = sem("w_ready"), sem("late_ready"), sem("ug_used"), sem("down_used")
        x1_loaded = [sem(f"x1_loaded{n}") for n in range(2)]
        x1_hi_ready, x1_lo_ready = sem("x1_hi_ready"), sem("x1_lo_ready")
        q_read, silu_ready, h_ready = sem("q_read"), sem("silu_ready"), sem("h_ready")
        t_done, hid_hi_ready, hid_lo_ready = sem("t_done"), sem("hid_hi_ready"), sem("hid_lo_ready")
        x1_turned, resid_ready, result_ready = sem("x1_turned"), sem("resid_ready"), sem("result_ready")
        stored = [sem(f"stored{n}") for n in range(2)]

        block = ctx.enter_context(nc.Block())

        def l0_piece(n):
            return slice(n * L0C, min((n + 1) * L0C, L0W))

        def xk(buf, k):
            return buf[:, :].rearrange("p (s k t) -> p s k t", s=GS, k=KD)[:, :, k, :]

        def chunk(buf, c):
            return buf[:, c * CH:(c + 1) * CH]

        def raw_chunk(c):
            return chunk(raw, c) if c < RING else chunk(raw_late, c - RING)

        def entry(eng, column, index, high):
            return eng.value_load(table[0:1, bass.ds(index + column, 1)], min_val=0, max_val=high)

        @block.sync
        def _(sp):
            sp.dma_start(l0_raw[:, l0_piece(0)], l0_w[:, l0_piece(0)]).then_inc(l0_loaded[0], 16)
            for k in range(KD):
                sp.dma_start(xk(xg[0], k), xk(x_t[0], k)).then_inc(x_first[k], 16)
                sp.dma_start(l0_raw[:, l0_piece(k + 1)], l0_w[:, l0_piece(k + 1)]).then_inc(l0_loaded[k + 1], 16)
            for n in range(1, XB):
                sp.dma_start(xg[n][:, :], x_t[n]).then_inc(x_loaded[n], 16)

            def load_chunk(run_expert, c, slot, into):
                sp.dma_start(into,
                             l1_w[bass.ds(run_expert, 1), :, c * CH:(c + 1) * CH].rearrange("a p n -> p (a n)"))\
                  .then_inc(raw_loaded[slot], 16)

            def load_bias(run_expert, offset):
                row = l1_b[bass.ds(run_expert, 1), :].to_broadcast([P, BIAS])
                sp.dma_start(bias[:, bass.ds(offset, BIAS)], row).then_inc(bias_loaded, 16)

            def load_x(g, n, stores):
                sp.wait_ge(x1_stored[n], 16 * stores)
                sp.dma_start(xg[n][:, :], x_t[g]).then_inc(x_loaded[n], 16)

            sp.wait_ge(table_ready, 1)
            first = entry(sp, T_EXPERT, 0, E - 1)
            for c in range(RING):
                load_chunk(first, c, c, chunk(raw, c))
            load_x(3, 0, 1)
            load_bias(first, 0)
            load_x(4, 1, 1)
            for c in range(RING, CHUNKS):
                sp.wait_ge(raw_free, c - RING + 1)
                load_chunk(first, c, c - RING, chunk(raw, c - RING))
                if c % 2 and c < CHUNKS - 1:
                    g = 5 + (c - RING) // 2
                    load_x(g, g % XB, g // XB)
            load_x(G - 1, (G - 1) % XB, (G - 1) // XB)
            runs = entry(sp, T_RUNS, 0, E)
            with sp.If(runs > 1):
                expert = entry(sp, T_EXPERT, 1, E - 1)
                sp.wait_ge(raw_free, CHUNKS)
                sp.wait_ge(x1_loaded[1], 16)
                for c in range(CHUNKS):
                    load_chunk(expert, c, c, raw_chunk(c))
                sp.wait_ge(x1_stored[2], 16 * 2)
                sp.wait_ge(bias_loaded, 16)
                load_bias(expert, BIAS)
            with sp.Fori(2, E) as r:
                with sp.If(runs > r):
                    expert = entry(sp, T_EXPERT, r, E - 1)
                    for c in range(CHUNKS):
                        if c < DV:
                            sp.wait_ge(raw_free, (r - 1) * DV + (PL + c + 1))
                        else:
                            sp.wait_ge(late_free, (r - 2) * PL + (c + 1 - DV))
                        load_chunk(expert, c, c, raw_chunk(c))
                    sp.wait_ge(bias_loaded, r * 16)
                    load_bias(expert, (r % 2) * BIAS)

        @block.gpsimd
        def _(pool):
            nc.gpsimd.memset(one[:, :], 1.0).then_inc(one_ready, 1)
            nc.gpsimd.iota(sort_rows_i[0:1, 0:E], pattern=[[-1, E]], base=E, channel_multiplier=0).then_inc(iota_ready, 1)
            nc.gpsimd.iota(sort_rows_i[0:1, B:2 * B], pattern=[[1, B]], base=0, channel_multiplier=0).then_inc(iota_ready, 1)
            nc.gpsimd.memset(ident[:, :], 0.0).then_inc(ident_ready, 1)
            pool.wait_ge(ident_ready, 1)
            nc.gpsimd.affine_select(out=ident[:, :], in_=ident[:, :], compare_op=ALU.not_equal, fill=1.0, base=0,
                                    pattern=[[-1, P]], channel_multiplier=1).then_inc(ident_ready, 1)

            def step(s):
                word = entry(pool, T_WORD, s, 255)
                with pool.If(word % 2 > 0):
                    for c in range(DV, CHUNKS):
                        pool.wait_ge(w_hi_ready, word // 16 * CHUNKS + (c + 1))
                        nc.gpsimd.tensor_tensor(chunk(w_lo, c), raw_chunk(c), chunk(w_hi, c).bitcast(F32), ALU.subtract)\
                          .then_inc(late_ready, 1)
                        if c > DV:
                            pool.wait_ge(late_ready, (s - 1) * PL + (c - DV))
                            pool.sem_inc(late_free, 1)
                    pool.wait_ge(late_ready, s * PL)
                    pool.sem_inc(late_free, 1)
                with pool.Else():
                    pool.sem_inc(late_ready, PL)

            pool.wait_ge(table_ready, 1)
            with pool.Fori(1, B) as s:
                step(s)

        @block.scalar
        def _(act):
            act.wait_ge(one_ready, 1)
            nc.scalar.activation(one[:, 0:1], one[:, 1:2], ACT.Silu).then_inc(one_used, 1)
            act.dma_start(cond[:, :], cond_row).then_inc(cond_loaded, 16)
            act.dma_start(lora_w[:, :], cond_t).then_inc(lora_w_loaded, 16)
            act.dma_start(base_b[:, :], l0_b).then_inc(base_b_loaded, 16)

            def x_high(g, n, k):
                nc.scalar.activation(xk(x_hi, k), xk(xg[n], k), ACT.Copy).then_inc(x_hi_ready, 1)

            def l0_high(n):
                act.wait_ge(l0_loaded[n], 16)
                nc.scalar.activation(l0_hi[:, l0_piece(n)], l0_raw[:, l0_piece(n)], ACT.Copy).then_inc(l0_hi_ready, 1)

            def next_x_high(g, n, k):
                act.wait_ge(x_used, (g - 1) * KD + (k + 1))
                x_high(g, n, k)

            def first_run_high(i, n):
                act.wait_ge(raw_loaded[n], i * 16 + 16)
                nc.scalar.activation(w_hi[:, bass.ds(i * (RING * CH) + n * CH, CH)], chunk(raw, n), ACT.Copy)\
                  .then_inc(w_hi_ready, 1)

            def low_high(g):
                act.wait_ge(low_scaled, g + 1)
                nc.scalar.activation(low_hi[:, :], low[:, :], ACT.Copy).then_inc(low_hi_ready, 1)

            def store_x1(g, n, blocks=(0, KD)):
                act.wait_ge(x1_made, g * KD + blocks[1])
                cols = slice(blocks[0] * S, blocks[1] * S)
                act.dma_start(x1_dram[bass.ds(g * GS, GS), :, cols].rearrange("s p n -> p s n"),
                              xg[n][:, :].rearrange("p (s n) -> p s n", s=GS)[:, :, cols]).then_inc(x1_stored[n], 16)

            def group(g, n, loaded, weights=None):
                for k in range(KD - 1):
                    if k == 0:
                        act.wait_ge(x_loaded[(n + 1) % XB], loaded)
                    next_x_high(g + 1, (n + 1) % XB, k)
                low_high(g)
                next_x_high(g + 1, (n + 1) % XB, KD - 1)
                if weights is not None:
                    for k in range(2):
                        first_run_high(weights[0], weights[1] + k)
                store_x1(g, n)

            for k in range(KD):
                l0_high(k)
                act.wait_ge(x_first[k], 16)
                x_high(0, 0, k)
            l0_high(KD)
            group(0, 0, 16)
            with act.Fori(0, (G - 2) // XB) as i:
                for n in range(XB):
                    group(i * XB + (n + 1), (n + 1) % XB, i * 16 + (32 if n == 2 else 16), weights=(i, 2 * n))
            act.wait_ge(x1_stored[0], 16)
            act.dma_start(x1[0][:, :], x1_dram[0]).then_inc(x1_loaded[0], 16)
            low_high(G - 1)

            act.sem_inc(stored[0], 16)
            act.sem_inc(stored[1], 16)

            def load_x1(s, n):
                sample = entry(act, T_SAMPLE, s, B - 1)
                act.dma_start(x1[n][:, :], x1_dram[bass.ds(sample, 1)].rearrange("a p n -> p (a n)")).then_inc(x1_loaded[n], 16)

            def x1_high(s, n, used=True):
                act.wait_ge(x1_loaded[n], (s - n) * 8 + 16)
                if used:
                    act.wait_ge(ug_used, (s - 1) * UG)
                nc.scalar.activation(x1_split[n][:, 0:D], x1[n][:, :], ACT.Copy).then_inc(x1_hi_ready, 1)

            def hidden_high(s, half):
                act.wait_ge(t_done, s * 2 + (half + 1))
                cols = slice(half * N, (half + 1) * N)
                nc.scalar.activation(hid_hi[:, cols], t_ps[half][:, :], ACT.Copy).then_inc(hid_hi_ready, 1)

            def silu(s, half, free):
                act.wait_ge(q_read, s * 4 + (2 * half + 1))
                if free:
                    act.wait_ge(h_ready, s * 2 + half)
                nc.scalar.activation(act_up[:, :], pre[:, :], ACT.Silu).then_inc(silu_ready, 1)

            def store(s, n):
                sample = entry(act, T_SAMPLE, s, B - 1)
                act.wait_ge(result_ready, s + 1)
                act.dma_start(out[bass.ds(sample, 1)].rearrange("a t d -> t (a d)"), result[n][:, :]).then_inc(stored[n], 16)

            def high_parts(changed, runs_before, index, chunks):
                with act.If(changed > 0):
                    for c in chunks:
                        act.wait_ge(raw_loaded[c], runs_before * 16 + (48 if c < RING else 16))
                        if c < UG:
                            act.wait_ge(ug_used, (index - 1) * UG + (c + 1))
                        else:
                            act.wait_ge(down_used, (index - 1) * DN + (c + 1 - UG))
                        nc.scalar.activation(chunk(w_hi, c), raw_chunk(c), ACT.Copy).then_inc(w_hi_ready, 1)

            def step(s, n, first=False, last=False, ahead_ends=False):
                silu(s, 0, not first)
                if first:
                    for m, stores in enumerate((3, 4, 2)):
                        act.wait_ge(x1_stored[m], 16 * stores)
                    load_x1(1, 1)
                else:
                    hidden_high(s - 1, 1)
                if not last:
                    x1_high(s + 1, 1 - n, used=not first)
                word = entry(act, T_WORD, s, 255)
                if not first:
                    last_run = entry(act, T_WORD, s - 1, 255) // 16
                    high_parts(word % 2, last_run, s, range(UG, UG + DN // 2))
                if not last:
                    high_parts(word // 4 % 2, word // 16, s + 1, range(0, 4))
                silu(s, 1, True)
                hidden_high(s, 0)
                if not first:
                    high_parts(word % 2, last_run, s, range(UG + DN // 2, CHUNKS))
                if not last:
                    high_parts(word // 8 % 2, word // 16, s + 1, range(0, 4))
                    high_parts(word // 2 % 2, word // 16, s + 1, range(4, UG))
                if not ahead_ends:
                    act.wait_ge(x1_turned, s * QUADS + QUADS)
                    act.wait_ge(x1_lo_ready, s + 1)
                    load_x1(s + 2, n)
                if not first and not last:
                    store(s - 1, 1 - n)

            act.wait_ge(x_used, G * KD)
            x1_high(0, 0, used=False)
            for blocks in ((0, KD // 2), (KD // 2, KD)):
                store_x1(G - 1, 1, blocks)
            step(0, 0, first=True)
            step(1, 1)
            with act.Fori(1, B // 2 - 1) as i:
                step(i * 2, 0)
                step(i * 2 + 1, 1)
            step(B - 2, 0, ahead_ends=True)
            step(B - 1, 1, last=True, ahead_ends=True)
            hidden_high(B - 1, 1)
            store(B - 2, 0)
            store(B - 1, 1)
            act.wait_ge(stored[0], 16 + 16 * B // 2)
            act.wait_ge(stored[1], 16 + 16 * B // 2)

        @block.vector
        def _(dve):
            done = [0]

            def then(instruction):
                done[0] += 1
                instruction.then_inc(table_step, 1)
                dve.wait_ge(table_step, done[0])

            def square(buf, a=B, b=B):
                return buf[0:1, 0:a * b].rearrange("p (a b) -> p a b", a=a)

            def outer(r, a=B, b=B):
                return r.unsqueeze(2).to_broadcast([1, a, b])

            def inner(r, a=B, b=B):
                return r.unsqueeze(1).to_broadcast([1, a, b])

            spare, key, other, ordered, index, few = [sort_rows[0:1, n * B:(n + 1) * B] for n in range(6)]
            down8, first8 = few[:, 0:E], few[:, E:E + 1]

            def sort_samples():
                dve.wait_ge(iota_ready, 2)
                dve.wait_ge(cond_loaded, 16)
                then(nc.vector.tensor_copy(down8, sort_rows_i[0:1, 0:E]))
                then(nc.vector.tensor_copy(index, sort_rows_i[0:1, B:2 * B]))
                cond3 = cond[:, :].rearrange("p (b e) -> p b e", b=B)
                then(nc.vector.tensor_reduce(spare, cond3, AX_X, ALU.max))
                then(nc.vector.tensor_tensor(square(wide[0], B, E), cond3, outer(spare, B, E), ALU.is_ge))
                then(nc.vector.tensor_tensor(square(wide[1], B, E), square(wide[0], B, E), inner(down8, B, E), ALU.mult))
                then(nc.vector.tensor_reduce(spare, square(wide[1], B, E), AX_X, ALU.max))
                then(nc.vector.tensor_scalar(spare, spare, 1.0, None, ALU.max))
                then(nc.vector.tensor_copy(first8, spare[:, 0:1]))
                then(nc.vector.tensor_tensor(spare, spare, first8.to_broadcast([1, B]), ALU.subtract))
                then(nc.vector.tensor_scalar(other, spare, 0.0, -float(B * E), ALU.is_gt, ALU.mult))
                then(nc.vector.scalar_tensor_tensor(key, spare, float(B), other, ALU.mult, ALU.add))
                then(nc.vector.tensor_tensor(key, key, index, ALU.subtract))
                left = [key, other]
                for n in range(B // 8):
                    top = ordered[:, 8 * n:8 * n + 8]
                    then(nc.vector.max(top, left[n % 2]))
                    then(nc.vector.match_replace(left[(n + 1) % 2], top, left[n % 2], -1e9))

            def make_table():
                then(nc.vector.tensor_scalar(spare, ordered, -1.0, None, ALU.mult))
                keys_i, behind_i = sort_rows_i[0:1, 2 * B:3 * B], sort_rows_i[0:1, 3 * B:4 * B]
                then(nc.vector.tensor_copy(keys_i, spare))
                then(nc.vector.tensor_single_scalar(table[0:1, T_SAMPLE:T_SAMPLE + B], keys_i, B - 1, ALU.bitwise_and))
                then(nc.vector.tensor_single_scalar(behind_i, keys_i, 5, ALU.arith_shift_right))
                behind, changed, run, shifted, after = ordered, key, other, spare, cond[0:1, 0:B]
                then(nc.vector.tensor_copy(behind, behind_i))
                then(nc.vector.memset(changed, 0.0))
                then(nc.vector.tensor_tensor(changed[:, 1:B], behind[:, 1:B], behind[:, 0:B - 1], ALU.not_equal))
                then(nc.vector.tensor_copy(run, changed))
                for n in range(5):
                    by = 2 ** n
                    then(nc.vector.tensor_copy(shifted, run))
                    then(nc.vector.tensor_tensor(run[:, by:B], shifted[:, by:B], shifted[:, 0:B - by], ALU.add))
                then(nc.vector.memset(after, 0.0))
                then(nc.vector.tensor_copy(after[:, 0:B - 1], changed[:, 1:B]))
                then(nc.vector.scalar_tensor_tensor(shifted, run, 16.0, changed, ALU.mult, ALU.add))
                then(nc.vector.tensor_tensor(changed, changed, after, ALU.mult))
                then(nc.vector.scalar_tensor_tensor(shifted, after, 6.0, shifted, ALU.mult, ALU.add))
                then(nc.vector.scalar_tensor_tensor(shifted, changed, 4.0, shifted, ALU.mult, ALU.add))
                then(nc.vector.tensor_copy(table[0:1, T_WORD:T_WORD + B], shifted))
                then(nc.vector.tensor_scalar(table[0:1, T_RUNS:T_RUNS + 1], run[:, B - 1:B], 1.0, None, ALU.add))
                of_run = after[:, 0:E]
                then(nc.vector.tensor_tensor(square(wide[0], E, B), outer(index[:, 0:E], E, B), inner(run, E, B), ALU.is_equal))
                then(nc.vector.tensor_tensor(square(wide[1], E, B), square(wide[0], E, B), inner(behind, E, B), ALU.mult))
                then(nc.vector.tensor_reduce(of_run, square(wide[1], E, B), AX_X, ALU.max))
                then(nc.vector.tensor_tensor(of_run, of_run, first8.to_broadcast([1, E]), ALU.subtract))
                then(nc.vector.tensor_scalar(of_run, of_run, float(E), None, ALU.add))
                then(nc.vector.tensor_copy(keys_i[:, 0:E], of_run))
                nc.vector.tensor_single_scalar(table[0:1, T_EXPERT:T_EXPERT + E], keys_i[:, 0:E], E - 1, ALU.bitwise_and)\
                  .then_inc(table_ready, 1)

            def subtract(lo, whole, hi):
                return nc.vector.tensor_tensor(lo, whole, hi.bitcast(F32), ALU.subtract)

            def l0_low(n):
                dve.wait_ge(l0_hi_ready, n + 1)
                subtract(l0_lo[:, l0_piece(n)], l0_raw[:, l0_piece(n)], l0_hi[:, l0_piece(n)]).then_inc(l0_lo_ready, 1)

            def x_low(g, n, k):
                dve.wait_ge(x_hi_ready, g * KD + (k + 1))
                subtract(xk(x_lo, k), xk(xg[n], k), xk(x_hi, k)).then_inc(x_lo_ready, 1)

            def w_low(c, whole):
                at_c = bass.ds(c * CH, CH)
                subtract(w_lo[:, at_c], whole, w_hi[:, at_c]).then_inc(w_ready, 1)

            def first_run_low(i, n):
                dve.wait_ge(w_hi_ready, i * RING + (n + 1))
                w_low(i * RING + n, chunk(raw, n))
                dve.wait_ge(w_ready, i * RING + (n + 1))
                dve.sem_inc(raw_free, 1)

            def x1_low(s, n):
                dve.wait_ge(x1_hi_ready, s + 1)
                subtract(x1_split[n][:, D:2 * D], x1[n][:, :], x1_split[n][:, 0:D]).then_inc(x1_lo_ready, 1)

            def group(g, n, weights=None, first=False, last=False):
                if first:
                    sort_samples()
                elif not last:
                    for k in range(KD - 2):
                        x_low(g + 1, (n + 1) % XB, k)
                dve.wait_ge(low_done, g + 1)
                if not first:
                    dve.wait_ge(low_lo_ready, g)
                nc.vector.tensor_tensor(low[:, :].rearrange("p (s t) -> p s t", s=GS),
                                        low_ps[:, :].rearrange("p (s t) -> p s t", s=GS),
                                        lora_w[:, bass.ds(g * GS, GS)].unsqueeze(2).to_broadcast([P, GS, S]),
                                        ALU.mult).then_inc(low_scaled, 1)
                if not first and not last:
                    x_low(g + 1, (n + 1) % XB, KD - 2)
                dve.wait_ge(low_hi_ready, g + 1)
                subtract(low_lo[:, :], low[:, :], low_hi[:, :]).then_inc(low_lo_ready, 1)
                if not last:
                    for k in range(0 if first else KD - 1, KD):
                        x_low(g + 1, (n + 1) % XB, k)
                for m in range(KD):
                    if last and m == 1:
                        x1_low(0, 0)
                    dve.wait_ge(base_done, g * KD + (m + 1))
                    nc.vector.scalar_tensor_tensor(xk(xg[n], m), q_ps[m][:, :].rearrange("p (s t) -> p s t", s=GS),
                                                   base_b[:, m:m + 1], xk(xg[n], m), ALU.add, ALU.add)\
                      .then_inc(x1_made, 1)
                if first:
                    make_table()
                if weights is not None:
                    for k in range(2):
                        first_run_low(weights[0], weights[1] + k)

            for k in range(KD):
                l0_low(k)
                x_low(0, 0, k)
            l0_low(KD)
            dve.wait_ge(lora_w_loaded, 16)
            nc.vector.tensor_scalar(lora_w[:, :], lora_w[:, :], LORA_SCALE, None, ALU.mult).then_inc(lora_w_loaded, 1)
            dve.wait_ge(lora_w_loaded, 17)
            dve.wait_ge(base_b_loaded, 16)
            group(0, 0, first=True)
            with dve.Fori(0, (G - 2) // XB) as i:
                for n in range(XB):
                    group(i * XB + (n + 1), (n + 1) % XB, weights=(i, 2 * n))
            group(G - 1, 1, last=True)

            def add_bias(s, q, dst, run, wait_bias=False):
                if wait_bias:
                    dve.wait_ge(bias_loaded, run * 16 + 16)
                dve.wait_ge(ug_used, s * UG + (2 * q + 2))
                nc.vector.tensor_tensor(dst[:, :], q_ps[q][:, :], bias[:, bass.ds((run % 2) * BIAS + q * N, N)], ALU.add)\
                  .then_inc(q_read, 1)

            def gated(s, half):
                dve.wait_ge(q_read, s * 4 + (2 * half + 2))
                dve.wait_ge(silu_ready, s * 2 + (half + 1))
                nc.vector.tensor_tensor(hidden[half][:, :], gate[:, :], act_up[:, :], ALU.mult).then_inc(h_ready, 1)

            def hidden_low(s, half):
                dve.wait_ge(hid_hi_ready, s * 2 + (half + 1))
                cols = slice(half * N, (half + 1) * N)
                subtract(hid_lo[:, cols], t_ps[half][:, :], hid_hi[:, cols]).then_inc(hid_lo_ready, 1)

            def finish(s, n, product=d_ps):
                dve.wait_ge(stored[n], (s - n) * 8 + 16)
                dve.wait_ge(resid_ready, s + 1)
                dve.wait_ge(down_used, s * DN + DN)
                nc.vector.tensor_tensor(result[n][:, :], product[:, :], resid[n][:, :], ALU.add).then_inc(result_ready, 1)

            def turn_x1(s, n, blocks):
                for b in blocks:
                    i, j = (slice(QUAD * q, QUAD * q + QUAD) for q in (b // (P // QUAD), b % (P // QUAD)))
                    nc.vector.transpose(resid[n][j, :].rearrange("p (k f) -> p k f", k=KD)[:, :, i],
                                        x1[n][i, :].rearrange("p (k t) -> p k t", k=KD)[:, :, j]).then_inc(x1_turned, 1)

            def residual(s, n, run):
                dve.wait_ge(x1_turned, s * QUADS + QUADS)
                nc.vector.tensor_tensor(resid[n][:, :], resid[n][:, :], bias[:, bass.ds((run % 2) * BIAS + 4 * N, N)], ALU.add)\
                  .then_inc(resid_ready, 1)

            def low_parts(run, index, chunks):
                for c in chunks:
                    dve.wait_ge(w_hi_ready, run * CHUNKS + (c + 1))
                    w_low(c, raw_chunk(c))
                    if c > chunks[0]:
                        dve.wait_ge(w_ready, index * DV + (PL + c))
                        dve.sem_inc(raw_free, 1)
                dve.wait_ge(w_ready, index * DV + (PL + chunks[-1] + 1))
                dve.sem_inc(raw_free, 1)

            def step(s, n, start=None, last=False):
                word = entry(dve, T_WORD, s, 255)
                run = dve.snap(word // 16)
                dve.wait_ge(x1_loaded[n], (s - n) * 8 + 16)
                if start is None:
                    dve.wait_ge(result_ready, s - 1)
                turn_x1(s, n, range(0, 4))
                add_bias(s, 0, pre, run, wait_bias=True)
                turn_x1(s, n, range(4, 12))
                if start != 0:
                    hidden_low(s - 1, 1)
                    dve.wait_ge(h_ready, s * 2)
                add_bias(s, 1, gate, run)
                gated(s, 0)
                if not last:
                    x1_low(s + 1, 1 - n)
                if not last:
                    with dve.If(word // 2 % 2 > 0):
                        with dve.If(word // 4 % 2 > 0):
                            low_parts(run + 1, s + 1, range(0, 4))
                    with dve.Else():
                        dve.sem_inc(w_ready, DV)
                add_bias(s, 2, pre, run)
                turn_x1(s, n, range(12, QUADS))
                if start != 0 and not last:
                    finish(s - 1, 1 - n)
                hidden_low(s, 0)

                def last_quarter():
                    dve.wait_ge(h_ready, s * 2 + 1)
                    add_bias(s, 3, gate, run)
                    gated(s, 1)
                    residual(s, n, run)

                if last:
                    last_quarter()
                    finish(s - 1, 1 - n)
                else:
                    with dve.If(word // 2 % 2 > 0):
                        with dve.If(word // 8 % 2 > 0):
                            low_parts(run + 1, s + 1, range(0, 4))
                        last_quarter()
                        low_parts(run + 1, s + 1, range(4, DV))
                    with dve.Else():
                        last_quarter()

            step(0, 0, start=0)
            step(1, 1, start=1)
            with dve.Fori(1, B // 2 - 1) as i:
                step(i * 2, 0)
                step(i * 2 + 1, 1)
            step(B - 2, 0)
            step(B - 1, 1, last=True)
            hidden_low(B - 1, 1)
            finish(B - 1, 1, last_d_ps)

        @block.tensor
        def _(pe):
            def product(dst, still_hi, still_lo, moving_hi, moving_lo, first, last):
                nc.tensor.matmul(dst, still_hi, moving_hi, start=first, stop=False)
                nc.tensor.matmul(dst, still_hi, moving_lo, start=False, stop=False)
                return nc.tensor.matmul(dst, still_lo, moving_hi, start=False, stop=last)

            def group(g, n, first=False):
                for k in range(KD):
                    if first:
                        pe.wait_ge(l0_lo_ready, k + 1)
                    pe.wait_ge(x_lo_ready, g * KD + (k + 1))
                    x_parts = xk(x_hi, k), xk(x_lo, k)
                    a = slice(k * L0C, k * L0C + ER)
                    if k == 0 and not first:
                        pe.wait_ge(low_scaled, g)
                    got = product(low_ps[:, :].rearrange("p (s t) -> p s t", s=GS), l0_hi[:, a], l0_lo[:, a], *x_parts, k == 0, k == KD - 1)
                    if k == KD - 1:
                        got.then_inc(low_done, 1)
                    for m in range(KD):
                        if k == 0 and not first:
                            pe.wait_ge(x1_made, g * KD + (m + 1 - KD))
                        w = slice(k * L0C + ER + m * P, k * L0C + ER + (m + 1) * P)
                        got = product(q_ps[m][:, :].rearrange("p (s t) -> p s t", s=GS), l0_hi[:, w], l0_lo[:, w], *x_parts, k == 0, False)
                    got.then_inc(x_used, 1)
                if first:
                    pe.wait_ge(l0_lo_ready, KD + 1)
                pe.wait_ge(low_lo_ready, g + 1)
                for m in range(KD):
                    w = slice(KD * L0C + m * P, KD * L0C + (m + 1) * P)
                    product(q_ps[m][:, :], l0_hi[:, w], l0_lo[:, w], low_hi[:, :], low_lo[:, :], False, True).then_inc(base_done, 1)

            pe.wait_ge(ident_ready, 2)
            for n in range(WARM):
                nc.tensor.matmul(low_ps[:, 0:P], ident[:, :], ident[:, :], start=True, stop=True)
            group(0, 0, first=True)
            with pe.Fori(1, G) as g:
                group(g, None)

            def low_part(s, c, step0):
                if step0:
                    pe.wait_ge(w_ready, c + 1)
                elif c < DV:
                    pe.wait_ge(w_ready, s * DV + (PL + c + 1))
                else:
                    pe.wait_ge(late_ready, (s - 1) * PL + (c + 1 - DV))

            def quarter(s, n, q, first):
                if q == 0:
                    pe.wait_ge(x1_lo_ready, s + 1)
                if first:
                    pe.wait_ge(x1_made, (G - 1) * KD + (q + 1))
                else:
                    pe.wait_ge(q_read, s * 4 + (q - 3))
                for c in range(2 * q, 2 * q + 2):
                    low_part(s, c, first)
                    for k in range(2 * (c % 2), 2 * (c % 2) + 2):
                        f = slice(k * P, (k + 1) * P)
                        fl = slice(D + k * P, D + (k + 1) * P)
                        w = slice((4 * q + k) * N, (4 * q + k + 1) * N)
                        got = product(q_ps[q][:, :], x1_split[n][:, f], x1_split[n][:, fl], w_hi[:, w], w_lo[:, w], k == 0, k == KD - 1)
                    got.then_inc(ug_used, 1)

            def transpose(dst, src, blocks):
                for k in range(blocks):
                    got = nc.tensor.transpose(dst[:, k * P:(k + 1) * P], src[:, k * P:(k + 1) * P], ident[:, :])
                return got

            def transpose_hidden(s, half, reused):
                pe.wait_ge(h_ready, s * 2 + (half + 1))
                if reused:
                    pe.wait_ge(hid_lo_ready, s * 2 + (half - 1))
                transpose(t_ps[half], hidden[half], KD).then_inc(t_done, 1)

            def down(s, chunks=range(DN), step0=False, dst=d_ps):
                for c in chunks:
                    low_part(s, UG + c, step0)
                    if c % 2 == 0:
                        pe.wait_ge(hid_lo_ready, s * 2 + (c // 2 + 1))
                    for k in range(2 * c, 2 * c + 2):
                        f = slice(k * P, (k + 1) * P)
                        w = slice((2 * UG + k) * N, (2 * UG + k + 1) * N)
                        got = product(dst[:, :], hid_hi[:, f], hid_lo[:, f], w_hi[:, w], w_lo[:, w], k == 0, k == KH - 1)
                    got.then_inc(down_used, 1)

            def step(s, n, last=False, start=None):
                quarter(s, n, 0, start == 0)
                if start != 0:
                    if start != 1:
                        pe.wait_ge(result_ready, s - 1)
                    down(s - 1, range(0, DN // 2), step0=start == 1)
                    transpose_hidden(s - 1, 1, start != 1)
                quarter(s, n, 1, start == 0)
                quarter(s, n, 2, start == 0)
                if start != 0 and not last:
                    down(s - 1, range(DN // 2, DN), step0=start == 1)
                transpose_hidden(s, 0, start != 0)
                quarter(s, n, 3, start == 0)
                if last:
                    down(s - 1, range(DN // 2, DN))

            step(0, 0, start=0)
            step(1, 1, start=1)
            with pe.Fori(1, B // 2 - 1) as i:
                step(i * 2, 0)
                step(i * 2 + 1, 1)
            step(B - 2, 0)
            step(B - 1, 1, last=True)
            transpose_hidden(B - 1, 1, True)
            down(B - 1, dst=last_d_ps)


def kernel(x, cond_8, L0_cond_W_base, L0_cond_b_base, L0_cond_As, L0_cond_Bs, L1_cond_W_up, L1_cond_b_up,
           L1_cond_W_gate, L1_cond_b_gate, L1_cond_W_down, L1_cond_b_down):
    import numpy as np
    import concourse.bacc as bacc
    from concourse.bass_utils import run_bass_kernel_spmd

    x, cond = np.asarray(x), np.asarray(cond_8)
    x_t = x.reshape(G, GS, S, KD, P).transpose(0, 4, 1, 3, 2).reshape(G, P, GS * D)
    a_t = np.asarray(L0_cond_As).reshape(ER, KD, P).transpose(2, 1, 0)
    base_t = np.asarray(L0_cond_W_base).reshape(D, KD, P).transpose(2, 1, 0)
    b_t = np.asarray(L0_cond_Bs).transpose(0, 2, 1).reshape(ER, D)
    l0_w = np.concatenate([np.concatenate([a_t, base_t], axis=2).reshape(P, KD * L0C), b_t], axis=1)
    l0_b = np.asarray(L0_cond_b_base).reshape(KD, P).T

    def halves(w):
        return np.asarray(w).reshape(E, H // N, N, KD, P).transpose(0, 4, 1, 3, 2)

    up, gate = halves(L1_cond_W_up), halves(L1_cond_W_gate)
    down = np.asarray(L1_cond_W_down).reshape(E, D, KH, P).transpose(0, 3, 2, 1)
    parts = [up[:, :, 0], gate[:, :, 0], up[:, :, 1], gate[:, :, 1], down]
    l1_w = np.concatenate(parts, axis=2).reshape(E, P, BLOCKS * N)
    bu, bg, bd = np.asarray(L1_cond_b_up), np.asarray(L1_cond_b_gate), np.asarray(L1_cond_b_down)
    l1_b = np.concatenate([bu[:, :N], bg[:, :N], bu[:, N:], bg[:, N:], bd], axis=1)
    arrays = {
        "x_t": x_t, "cond_row": cond.reshape(1, B * E), "cond_t": np.repeat(cond.T, R, axis=0),
        "l0_w": l0_w, "l0_b": l0_b, "l1_w": l1_w, "l1_b": l1_b,
    }
    arrays = {name: np.ascontiguousarray(a) for name, a in arrays.items()}
    nc = bacc.Bacc("TRN2", target_bir_lowering=False, num_devices=1)
    args = [nc.dram_tensor(name, a.shape, mybir.dt.from_np(a.dtype), kind="ExternalInput").ap() for name, a in arrays.items()]
    out = nc.dram_tensor("out", (B, S, D), F32, kind="ExternalOutput").ap()
    program(nc, *args, out)
    result = run_bass_kernel_spmd(nc, [arrays], core_ids=[0])
    return result.results[0]["out"]
```
